# Optimizing a Trainium2 kernel written in Bass

```python
import numpy as np
import jax
import jax.numpy as jnp

def _softmax(x, axis=-1):
    return jax.nn.softmax(x, axis=axis)

def _gelu(x):
    return jax.nn.gelu(x, approximate=True)

def _silu(x):
    return jax.nn.silu(x)

def _sigmoid(x):
    return jax.nn.sigmoid(x)

def _layernorm(x, axis=-1, eps=1e-05):
    m = jnp.mean(x, axis=axis, keepdims=True)
    v = jnp.var(x, axis=axis, keepdims=True)
    return (x - m) / jnp.sqrt(v + eps)

def _scatter_add(tgt, idx, src, axis=0):
    return tgt.at[idx].add(src)

def _segment_sum(src, seg, n):
    return jax.ops.segment_sum(src, seg, n)
kernel_name = 'mk_prb_d4_jaxref_r8_ccf26f'

def setup_inputs(seed: int=0):
    np.random.seed(seed)
    _w = jnp.asarray

    def _L0_attn_setup():
        import jax, jax.numpy as jnp
        import numpy as np
        B, T, H = (2, 512, 256)
        NH, DK, DV = (16, 128, 128)
        CONV = 4
        MLP_H = 32
        EPS_STAT = 1e-06
        NORM_EPS = 1e-05
        L2_EPS = 1e-06

        def short_conv(x, w):
            K = w.shape[-1]
            xp = jnp.pad(x, ((0, 0), (K - 1, 0), (0, 0)))
            y = sum((xp[:, i:i + x.shape[1], :] * w[:, i] for i in range(K)))
            return jax.nn.silu(y)

        def _mlp(s, W1, b1, W2, b2):
            return (jax.nn.silu(s @ W1.T + b1) @ W2.T + b2)[..., 0]
        key = jax.random.key(seed)
        ks = jax.random.split(key, 20)

        def w(k, shape, scale=None):
            scale = 1.0 / np.sqrt(shape[-1]) if scale is None else scale
            return jax.random.normal(k, shape, jnp.float32) * scale
        return dict(hidden_states=jax.random.normal(ks[0], (B, T, H), jnp.float32), Wq=w(ks[1], (NH * DK, H)), Wk=w(ks[2], (NH * DK, H)), Wv=w(ks[3], (NH * DV, H)), conv_q=w(ks[4], (NH * DK, CONV), 0.5), conv_k=w(ks[5], (NH * DK, CONV), 0.5), conv_v=w(ks[6], (NH * DV, CONV), 0.5), A_log=jnp.log(jax.random.uniform(ks[7], (NH,), jnp.float32, 1.0, 16.0)), dt_bias=jnp.zeros((NH * DK,), jnp.float32), Wsv=w(ks[8], (DV, DK)), Wb1=w(ks[9], (MLP_H, 3)), bb1=jnp.zeros((MLP_H,), jnp.float32), Wb2=w(ks[10], (1, MLP_H)), bb2=jnp.zeros((1,), jnp.float32), Wa1=w(ks[11], (MLP_H, 3)), ba1=jnp.zeros((MLP_H,), jnp.float32), Wa2=w(ks[12], (1, MLP_H)), ba2=jnp.zeros((1,), jnp.float32), Wg1=w(ks[13], (DV, H)), Wg2=w(ks[14], (NH * DV, DV)), bg2=jnp.zeros((NH * DV,), jnp.float32), norm_w=jnp.ones((DV,), jnp.float32), Wo=w(ks[15], (H, NH * DV)))
    _L0_attn_in = _L0_attn_setup()

    def _L0_ffn_setup():
        import jax, jax.numpy as jnp
        import numpy as np
        EPS = 1e-08

        def _quantize(w):
            gamma = jnp.mean(jnp.abs(w))
            return jnp.clip(jnp.round(w / (gamma + EPS)), -1.0, 1.0)

        def _bitlinear(x, w):
            return jnp.matmul(x, _quantize(w).T)
        key = jax.random.key(seed)
        k1, k2, k3, k4 = jax.random.split(key, 4)
        d, h = (256, 704)
        x = jax.random.normal(k1, (4, 256, d), dtype=jnp.float32)
        w1 = jax.random.normal(k2, (h, d), dtype=jnp.float32)
        w2 = jax.random.normal(k3, (h, d), dtype=jnp.float32)
        w3 = jax.random.normal(k4, (d, h), dtype=jnp.float32)
        return {'x': x, 'w1': w1, 'w2': w2, 'w3': w3}
    _L0_ffn_in = _L0_ffn_setup()

    def _L1_attn_setup():
        import jax, jax.numpy as jnp
        import numpy as np
        B, S, HID = (2, 256, 256)
        NH, NKV, HD = (16, 4, 128)
        KV_DIM = NKV * HD
        key = jax.random.key(seed)
        ks = jax.random.split(key, 7)
        sc = 0.02
        return {'hidden_states': jax.random.normal(ks[0], (B, S, HID), dtype=jnp.float32), 'Wq': jax.random.normal(ks[1], (NH * HD, HID), dtype=jnp.float32) * sc, 'Wk': jax.random.normal(ks[2], (KV_DIM, HID), dtype=jnp.float32) * sc, 'Wv': jax.random.normal(ks[3], (KV_DIM, HID), dtype=jnp.float32) * sc, 'Wo': jax.random.normal(ks[4], (HID, NH * HD), dtype=jnp.float32) * sc, 'bo': jnp.zeros((HID,), dtype=jnp.float32)}
    _L1_attn_in = _L1_attn_setup()

    def _L1_ffn_setup():
        import jax, jax.numpy as jnp
        import numpy as np
        HIDDEN = 256
        INTER = 1024
        BATCH, LOCAL_SEQ = (2, 512)
        key = jax.random.key(seed)
        k1, k2, k3 = jax.random.split(key, 3)
        h_shard = jax.random.normal(k1, (BATCH, LOCAL_SEQ, HIDDEN), dtype=jnp.float32)
        w_gate_up = jax.random.normal(k2, (2 * INTER, HIDDEN), dtype=jnp.float32) * 0.02
        w_down = jax.random.normal(k3, (HIDDEN, INTER), dtype=jnp.float32) * 0.02
        return {'h_shard': h_shard, 'w_gate_up': w_gate_up, 'w_down': w_down}
    _L1_ffn_in = _L1_ffn_setup()

    def _L2_attn_setup():
        import jax, jax.numpy as jnp
        import numpy as np
        B, S, D = (4, 128, 256)
        H, G = (16, 2)
        HD = D // H

        def rotate_half(x):
            x1, x2 = (x[..., :x.shape[-1] // 2], x[..., x.shape[-1] // 2:])
            return jnp.concatenate([-x2, x1], axis=-1)
        key = jax.random.key(seed)
        ks = jax.random.split(key, 9)
        scale = 0.02
        return {'x': jax.random.normal(ks[0], (B, S, D), jnp.float32), 'wq': jax.random.normal(ks[1], (D, D), jnp.float32) * scale, 'bq': jnp.zeros((D,), jnp.float32), 'wk': jax.random.normal(ks[2], (D, G * HD), jnp.float32) * scale, 'bk': jnp.zeros((G * HD,), jnp.float32), 'wv': jax.random.normal(ks[3], (D, G * HD), jnp.float32) * scale, 'bv': jnp.zeros((G * HD,), jnp.float32), 'wo': jax.random.normal(ks[4], (D, D), jnp.float32) * scale, 'bo': jnp.zeros((D,), jnp.float32)}
    _L2_attn_in = _L2_attn_setup()

    def _L2_ffn_setup():
        import jax, jax.numpy as jnp
        import numpy as np
        E, TOP_K, H, I = (16, 2, 256, 128)
        B, S = (2, 256)
        GROUP = 16
        RSF = 1.0

        def _dequant(q, blocks_scale, global_scale):
            e, k, n = q.shape
            w = (q.astype(jnp.float32) - 8.0).reshape(e, k // GROUP, GROUP, n)
            w = w * blocks_scale[:, :, None, :]
            return w.reshape(e, k, n) * global_scale[0]
        key = jax.random.key(seed)
        ks = jax.random.split(key, 6)
        hidden_states = jax.random.normal(ks[0], (B, S, H), dtype=jnp.float32)
        gate_weight = jax.random.normal(ks[1], (E, H), dtype=jnp.float32) * 0.02
        fc_up_qweights = jax.random.randint(ks[2], (E, H, I), 0, 16, dtype=jnp.int32)
        fc_up_blocks_scale = jax.random.uniform(ks[3], (E, H // GROUP, I), dtype=jnp.float32) * 0.02
        fc_up_global_scale = jnp.ones((1,), dtype=jnp.float32)
        fc_down_qweights = jax.random.randint(ks[4], (E, I, H), 0, 16, dtype=jnp.int32)
        fc_down_blocks_scale = jax.random.uniform(ks[5], (E, I // GROUP, H), dtype=jnp.float32) * 0.02
        fc_down_global_scale = jnp.ones((1,), dtype=jnp.float32)
        return {'hidden_states': hidden_states, 'gate_weight': gate_weight, 'fc_up_blocks_scale': fc_up_blocks_scale, 'fc_up_global_scale': fc_up_global_scale, 'fc_down_blocks_scale': fc_down_blocks_scale, 'fc_down_global_scale': fc_down_global_scale, 'fc_up_qweights': fc_up_qweights, 'fc_down_qweights': fc_down_qweights}
    _L2_ffn_in = _L2_ffn_setup()

    def _L3_attn_setup():
        import jax, jax.numpy as jnp
        import numpy as np
        H = 32
        D = 64
        BS = 32
        LAYER_IDX = 0
        NUM_LAYERS = 32
        EPS = 1e-05

        def _decay_buffers():
            base = 1.0 / 2.0 ** (8.0 / H)
            rate = base ** (jnp.arange(H, dtype=jnp.float32) + 1.0)
            factor = 1.0 - LAYER_IDX / (NUM_LAYERS - 1 + 1e-05) + 1e-05
            slope = (rate * factor)[:, None, None]
            r = jnp.arange(BS, dtype=jnp.float32) + 1.0
            query_decay = jnp.exp(-slope * r[:, None])
            key_decay = jnp.exp(-slope * (BS - r[:, None]))
            dd = r[:, None] - r[None, :]
            dd = slope * dd[None, :, :]
            dd = jnp.where(dd >= 0, -dd, -jnp.inf)
            diagonal_decay = jnp.exp(dd)[None]
            block_decay = jnp.exp(-slope * BS)
            return (slope, query_decay, key_decay, diagonal_decay, block_decay)

        def _rmsnorm(x, w):
            v = jnp.mean(x.astype(jnp.float32) ** 2, axis=-1, keepdims=True)
            return (x * jax.lax.rsqrt(v + EPS)).astype(x.dtype) * w
        key = jax.random.key(seed)
        ks = jax.random.split(key, 4)
        b, s, hid = (2, 512, 256)
        return {'hidden_states': jax.random.normal(ks[0], (b, s, hid), jnp.float32), 'qkv_w': jax.random.normal(ks[1], (3 * H * D, hid), jnp.float32) * 0.02, 'out_w': jax.random.normal(ks[2], (hid, H * D), jnp.float32) * 0.02, 'gate_w': jax.random.normal(ks[3], (H * D, hid), jnp.float32) * 0.02, 'norm_w': jnp.ones((H * D,), jnp.float32)}
    _L3_attn_in = _L3_attn_setup()

    def _L3_ffn_setup():
        import jax, jax.numpy as jnp
        import numpy as np
        E = 8
        TOP_K = 2
        H = 256
        I = 176
        SI = 704
        key = jax.random.key(seed)
        ks = jax.random.split(key, 9)
        s = lambda fan_in: 1.0 / np.sqrt(fan_in)
        return {'hidden_states': jax.random.normal(ks[0], (4, 256, H), dtype=jnp.float32), 'router_w': jax.random.normal(ks[1], (E, H), dtype=jnp.float32) * s(H), 'w_gate': jax.random.normal(ks[2], (E, H, I), dtype=jnp.float32) * s(H), 'w_up': jax.random.normal(ks[3], (E, H, I), dtype=jnp.float32) * s(H), 'w_down': jax.random.normal(ks[4], (E, I, H), dtype=jnp.float32) * s(I), 'sw_gate': jax.random.normal(ks[5], (H, SI), dtype=jnp.float32) * s(H), 'sw_up': jax.random.normal(ks[6], (H, SI), dtype=jnp.float32) * s(H), 'sw_down': jax.random.normal(ks[7], (SI, H), dtype=jnp.float32) * s(SI), 'shared_gate_w': jax.random.normal(ks[8], (H,), dtype=jnp.float32) * s(H)}
    _L3_ffn_in = _L3_ffn_setup()
    _d = {'L0_attn_hidden_states': _L0_attn_in['hidden_states'], 'L0_attn_Wq': _L0_attn_in['Wq'], 'L0_attn_Wk': _L0_attn_in['Wk'], 'L0_attn_Wv': _L0_attn_in['Wv'], 'L0_attn_conv_q': _L0_attn_in['conv_q'], 'L0_attn_conv_k': _L0_attn_in['conv_k'], 'L0_attn_conv_v': _L0_attn_in['conv_v'], 'L0_attn_A_log': _L0_attn_in['A_log'], 'L0_attn_dt_bias': _L0_attn_in['dt_bias'], 'L0_attn_Wsv': _L0_attn_in['Wsv'], 'L0_attn_Wb1': _L0_attn_in['Wb1'], 'L0_attn_bb1': _L0_attn_in['bb1'], 'L0_attn_Wb2': _L0_attn_in['Wb2'], 'L0_attn_bb2': _L0_attn_in['bb2'], 'L0_attn_Wa1': _L0_attn_in['Wa1'], 'L0_attn_ba1': _L0_attn_in['ba1'], 'L0_attn_Wa2': _L0_attn_in['Wa2'], 'L0_attn_ba2': _L0_attn_in['ba2'], 'L0_attn_Wg1': _L0_attn_in['Wg1'], 'L0_attn_Wg2': _L0_attn_in['Wg2'], 'L0_attn_bg2': _L0_attn_in['bg2'], 'L0_attn_norm_w': _L0_attn_in['norm_w'], 'L0_attn_Wo': _L0_attn_in['Wo'], 'L0_ffn_w1': _L0_ffn_in['w1'], 'L0_ffn_w2': _L0_ffn_in['w2'], 'L0_ffn_w3': _L0_ffn_in['w3'], 'L1_attn_Wq': _L1_attn_in['Wq'], 'L1_attn_Wk': _L1_attn_in['Wk'], 'L1_attn_Wv': _L1_attn_in['Wv'], 'L1_attn_Wo': _L1_attn_in['Wo'], 'L1_attn_bo': _L1_attn_in['bo'], 'L1_ffn_w_gate_up': _L1_ffn_in['w_gate_up'], 'L1_ffn_w_down': _L1_ffn_in['w_down'], 'L2_attn_wq': _L2_attn_in['wq'], 'L2_attn_bq': _L2_attn_in['bq'], 'L2_attn_wk': _L2_attn_in['wk'], 'L2_attn_bk': _L2_attn_in['bk'], 'L2_attn_wv': _L2_attn_in['wv'], 'L2_attn_bv': _L2_attn_in['bv'], 'L2_attn_wo': _L2_attn_in['wo'], 'L2_attn_bo': _L2_attn_in['bo'], 'L2_ffn_gate_weight': _L2_ffn_in['gate_weight'], 'L2_ffn_fc_up_blocks_scale': _L2_ffn_in['fc_up_blocks_scale'], 'L2_ffn_fc_up_global_scale': _L2_ffn_in['fc_up_global_scale'], 'L2_ffn_fc_down_blocks_scale': _L2_ffn_in['fc_down_blocks_scale'], 'L2_ffn_fc_down_global_scale': _L2_ffn_in['fc_down_global_scale'], 'L2_ffn_fc_up_qweights': _L2_ffn_in['fc_up_qweights'], 'L2_ffn_fc_down_qweights': _L2_ffn_in['fc_down_qweights'], 'L3_attn_qkv_w': _L3_attn_in['qkv_w'], 'L3_attn_out_w': _L3_attn_in['out_w'], 'L3_attn_gate_w': _L3_attn_in['gate_w'], 'L3_attn_norm_w': _L3_attn_in['norm_w'], 'L3_ffn_router_w': _L3_ffn_in['router_w'], 'L3_ffn_w_gate': _L3_ffn_in['w_gate'], 'L3_ffn_w_up': _L3_ffn_in['w_up'], 'L3_ffn_w_down': _L3_ffn_in['w_down'], 'L3_ffn_sw_gate': _L3_ffn_in['sw_gate'], 'L3_ffn_sw_up': _L3_ffn_in['sw_up'], 'L3_ffn_sw_down': _L3_ffn_in['sw_down'], 'L3_ffn_shared_gate_w': _L3_ffn_in['shared_gate_w']}
    _x0 = _d['L0_attn_hidden_states']
    _d['L0_attn_hidden_states'] = jax.random.normal(jax.random.fold_in(jax.random.key(seed), 1), (2, 1024, 256), dtype=_x0.dtype)
    del _x0
    return _d

def reference(L0_attn_hidden_states, L0_attn_Wq, L0_attn_Wk, L0_attn_Wv, L0_attn_conv_q, L0_attn_conv_k, L0_attn_conv_v, L0_attn_A_log, L0_attn_dt_bias, L0_attn_Wsv, L0_attn_Wb1, L0_attn_bb1, L0_attn_Wb2, L0_attn_bb2, L0_attn_Wa1, L0_attn_ba1, L0_attn_Wa2, L0_attn_ba2, L0_attn_Wg1, L0_attn_Wg2, L0_attn_bg2, L0_attn_norm_w, L0_attn_Wo, L0_ffn_w1, L0_ffn_w2, L0_ffn_w3, L1_attn_Wq, L1_attn_Wk, L1_attn_Wv, L1_attn_Wo, L1_attn_bo, L1_ffn_w_gate_up, L1_ffn_w_down, L2_attn_wq, L2_attn_bq, L2_attn_wk, L2_attn_bk, L2_attn_wv, L2_attn_bv, L2_attn_wo, L2_attn_bo, L2_ffn_gate_weight, L2_ffn_fc_up_blocks_scale, L2_ffn_fc_up_global_scale, L2_ffn_fc_down_blocks_scale, L2_ffn_fc_down_global_scale, L2_ffn_fc_up_qweights, L2_ffn_fc_down_qweights, L3_attn_qkv_w, L3_attn_out_w, L3_attn_gate_w, L3_attn_norm_w, L3_ffn_router_w, L3_ffn_w_gate, L3_ffn_w_up, L3_ffn_w_down, L3_ffn_sw_gate, L3_ffn_sw_up, L3_ffn_sw_down, L3_ffn_shared_gate_w):

    def _L0_attn_ref(hidden_states, Wq, Wk, Wv, conv_q, conv_k, conv_v, A_log, dt_bias, Wsv, Wb1, bb1, Wb2, bb2, Wa1, ba1, Wa2, ba2, Wg1, Wg2, bg2, norm_w, Wo):
        import jax, jax.numpy as jnp
        import numpy as np
        B, T, H = (2, 512, 256)
        NH, DK, DV = (16, 128, 128)
        CONV = 4
        MLP_H = 32
        EPS_STAT = 1e-06
        NORM_EPS = 1e-05
        L2_EPS = 1e-06

        def short_conv(x, w):
            K = w.shape[-1]
            xp = jnp.pad(x, ((0, 0), (K - 1, 0), (0, 0)))
            y = sum((xp[:, i:i + x.shape[1], :] * w[:, i] for i in range(K)))
            return jax.nn.silu(y)

        def _mlp(s, W1, b1, W2, b2):
            return (jax.nn.silu(s @ W1.T + b1) @ W2.T + b2)[..., 0]
        x = hidden_states
        Bsz, Tlen, _ = x.shape
        q = short_conv(x @ Wq.T, conv_q).reshape(Bsz, Tlen, NH, DK)
        k = short_conv(x @ Wk.T, conv_k).reshape(Bsz, Tlen, NH, DK)
        v = short_conv(x @ Wv.T, conv_v).reshape(Bsz, Tlen, NH, DV)
        v_hat = jnp.einsum('bthk,vk->bthv', k, Wsv)
        e = v_hat - v
        s_l2 = jnp.sqrt(jnp.sum(e * e, -1) + EPS_STAT)
        s_l1 = jnp.sum(jnp.abs(e), -1)
        cos_den = jnp.sqrt(jnp.sum(v_hat * v_hat, -1) + EPS_STAT) * jnp.sqrt(jnp.sum(v * v, -1) + EPS_STAT) + EPS_STAT
        s_cos = 1.0 - jnp.sum(v_hat * v, -1) / cos_den
        s = jnp.stack([s_l2, s_l1, s_cos], -1)
        beta = jax.nn.sigmoid(_mlp(s, Wb1, bb1, Wb2, bb2))
        amp = _mlp(s, Wa1, ba1, Wa2, ba2)
        r = k / jnp.maximum(jnp.linalg.norm(k, axis=-1, keepdims=True), 1e-12)
        g_raw = r * amp[..., None]
        g = -jnp.exp(A_log)[None, None, :, None] * jax.nn.softplus(g_raw + dt_bias.reshape(NH, DK))
        qn = q * jax.lax.rsqrt(jnp.sum(q * q, -1, keepdims=True) + L2_EPS)
        kn = k * jax.lax.rsqrt(jnp.sum(k * k, -1, keepdims=True) + L2_EPS)
        scale = DK ** (-0.5)

        def step(S, inp):
            q_t, k_t, v_t, g_t, b_t = inp
            S = S * jnp.exp(g_t)[..., None]
            kv = jnp.einsum('bhk,bhkv->bhv', k_t, S)
            delta = (v_t - kv) * b_t[..., None]
            S = S + k_t[..., None] * delta[..., None, :]
            o_t = jnp.einsum('bhk,bhkv->bhv', q_t * scale, S)
            return (S, o_t)
        tfirst = lambda a: jnp.swapaxes(a, 0, 1)
        S0 = jnp.zeros((Bsz, NH, DK, DV), jnp.float32)
        _, o = jax.lax.scan(step, S0, (tfirst(qn), tfirst(kn), tfirst(v), tfirst(g), tfirst(beta)))
        o = jnp.swapaxes(o, 0, 1)
        gate = (x @ Wg1.T @ Wg2.T + bg2).reshape(Bsz, Tlen, NH, DV)
        o = o * jax.lax.rsqrt(jnp.mean(o * o, -1, keepdims=True) + NORM_EPS) * norm_w
        o = o * jax.nn.sigmoid(gate)
        return o.reshape(Bsz, Tlen, NH * DV) @ Wo.T

    def _L0_ffn_ref(x, w1, w2, w3):
        import jax, jax.numpy as jnp
        import numpy as np
        EPS = 1e-08

        def _quantize(w):
            gamma = jnp.mean(jnp.abs(w))
            return jnp.clip(jnp.round(w / (gamma + EPS)), -1.0, 1.0)

        def _bitlinear(x, w):
            return jnp.matmul(x, _quantize(w).T)
        x1 = _bitlinear(x, w1)
        x2 = _bitlinear(x, w2)
        hidden = jax.nn.sigmoid(x1) * x2
        return _bitlinear(hidden, w3)

    def _L1_attn_ref(hidden_states, Wq, Wk, Wv, Wo, bo):
        import jax, jax.numpy as jnp
        import numpy as np
        B, S, HID = (2, 256, 256)
        NH, NKV, HD = (16, 4, 128)
        KV_DIM = NKV * HD
        b, s, _ = hidden_states.shape
        q = (hidden_states @ Wq.T).reshape(b, s, NH, HD).transpose(0, 2, 1, 3)
        k = (hidden_states @ Wk.T).reshape(b, s, NKV, HD).transpose(0, 2, 1, 3)
        v = (hidden_states @ Wv.T).reshape(b, s, NKV, HD).transpose(0, 2, 1, 3)
        g = NH // NKV
        k_rep = jnp.repeat(k, g, axis=1)
        v_rep = jnp.repeat(v, g, axis=1)
        qf = q.astype(jnp.float32)
        kf = k_rep.astype(jnp.float32)
        scores = jnp.einsum('bhqd,bhkd->bhqk', qf, kf)
        causal = jnp.tril(jnp.ones((s, s), dtype=bool))[None, None]
        neg = jnp.finfo(scores.dtype).min
        scores = jnp.where(causal, scores, neg)
        attn = jax.nn.softmax(scores, axis=-1).astype(v.dtype)
        out = jnp.einsum('bhqk,bhkd->bhqd', attn, v_rep)
        out = out.transpose(0, 2, 1, 3).reshape(b, s, NH * HD)
        return out @ Wo.T + bo

    def _L1_ffn_ref(h_shard, w_gate_up, w_down):
        import jax, jax.numpy as jnp
        import numpy as np
        HIDDEN = 256
        INTER = 1024
        BATCH, LOCAL_SEQ = (2, 512)
        batch, local_seq, hidden = h_shard.shape
        gate_up = jnp.einsum('bsh,oh->bso', h_shard, w_gate_up)
        gate, up = jnp.split(gate_up, 2, axis=-1)
        h = jax.nn.silu(gate) * up
        out = jnp.einsum('bsi,hi->bsh', h, w_down)
        return out

    def _L2_attn_ref(x, wq, bq, wk, bk, wv, bv, wo, bo):
        import jax, jax.numpy as jnp
        import numpy as np
        B, S, D = (4, 128, 256)
        H, G = (16, 2)
        HD = D // H

        def rotate_half(x):
            x1, x2 = (x[..., :x.shape[-1] // 2], x[..., x.shape[-1] // 2:])
            return jnp.concatenate([-x2, x1], axis=-1)
        b, s, d = x.shape
        hd = HD
        q = (x @ wq + bq).reshape(b, s, H, hd)
        k = (x @ wk + bk).reshape(b, s, G, hd)
        v = (x @ wv + bv).reshape(b, s, G, hd)
        inv_freq = 1.0 / 1250 ** (jnp.arange(0, hd, 2, dtype=jnp.float32) / hd)
        t = jnp.arange(s, dtype=jnp.float32)
        freqs = jnp.outer(t, inv_freq)
        freqs = jnp.concatenate([freqs, freqs], -1)
        sin = jnp.sin(freqs)[:, None, :]
        cos = jnp.cos(freqs)[:, None, :]
        q = q * cos + rotate_half(q) * sin
        q = q * hd ** (-0.5)
        k = k * cos + rotate_half(k) * sin
        reps = H // G
        k_exp = jnp.repeat(k, reps, axis=2)
        v_exp = jnp.repeat(v, reps, axis=2)
        scores = jnp.einsum('bqhd,bkhd->bhqk', q, k_exp) * hd ** (-0.5)
        attn = jax.nn.softmax(scores, axis=-1)
        out = jnp.einsum('bhqk,bkhd->bqhd', attn, v_exp).reshape(b, s, d)
        return out @ wo + bo

    def _L2_ffn_ref(hidden_states, gate_weight, fc_up_blocks_scale, fc_up_global_scale, fc_down_blocks_scale, fc_down_global_scale, fc_up_qweights, fc_down_qweights):
        import jax, jax.numpy as jnp
        import numpy as np
        E, TOP_K, H, I = (16, 2, 256, 128)
        B, S = (2, 256)
        GROUP = 16
        RSF = 1.0

        def _dequant(q, blocks_scale, global_scale):
            e, k, n = q.shape
            w = (q.astype(jnp.float32) - 8.0).reshape(e, k // GROUP, GROUP, n)
            w = w * blocks_scale[:, :, None, :]
            return w.reshape(e, k, n) * global_scale[0]
        b, s, h = hidden_states.shape
        x = hidden_states.reshape(-1, h).astype(jnp.float32)
        t = x.shape[0]
        logits = jax.nn.log_sigmoid(x @ gate_weight.T)
        probs = jax.nn.softmax(logits, axis=-1)
        topw, topi = jax.lax.top_k(probs, TOP_K)
        topw = topw / (jnp.sum(topw, axis=-1, keepdims=True) + 1e-20)
        wdense = jnp.zeros((t, E), dtype=jnp.float32)
        wdense = wdense.at[jnp.arange(t)[:, None], topi].add(topw) * RSF
        w_up = _dequant(fc_up_qweights, fc_up_blocks_scale, fc_up_global_scale)
        w_down = _dequant(fc_down_qweights, fc_down_blocks_scale, fc_down_global_scale)
        z = jnp.einsum('th,ehi->tei', x, w_up)
        a = jnp.square(jnp.maximum(z, 0.0))
        aw = a * wdense[:, :, None]
        y = jnp.einsum('tei,eih->th', aw, w_down)
        return y.reshape(b, s, h)

    def _L3_attn_ref(hidden_states, qkv_w, out_w, gate_w, norm_w):
        import jax, jax.numpy as jnp
        import numpy as np
        H = 32
        D = 64
        BS = 32
        LAYER_IDX = 0
        NUM_LAYERS = 32
        EPS = 1e-05

        def _decay_buffers():
            base = 1.0 / 2.0 ** (8.0 / H)
            rate = base ** (jnp.arange(H, dtype=jnp.float32) + 1.0)
            factor = 1.0 - LAYER_IDX / (NUM_LAYERS - 1 + 1e-05) + 1e-05
            slope = (rate * factor)[:, None, None]
            r = jnp.arange(BS, dtype=jnp.float32) + 1.0
            query_decay = jnp.exp(-slope * r[:, None])
            key_decay = jnp.exp(-slope * (BS - r[:, None]))
            dd = r[:, None] - r[None, :]
            dd = slope * dd[None, :, :]
            dd = jnp.where(dd >= 0, -dd, -jnp.inf)
            diagonal_decay = jnp.exp(dd)[None]
            block_decay = jnp.exp(-slope * BS)
            return (slope, query_decay, key_decay, diagonal_decay, block_decay)

        def _rmsnorm(x, w):
            v = jnp.mean(x.astype(jnp.float32) ** 2, axis=-1, keepdims=True)
            return (x * jax.lax.rsqrt(v + EPS)).astype(x.dtype) * w
        b, s, hid = hidden_states.shape
        nb = s // BS
        _, qd, kd, dd, bd = _decay_buffers()
        qkv = jax.nn.silu(hidden_states @ qkv_w.T)
        qkv = qkv.reshape(b, s, H, 3 * D)
        q, k, v = jnp.split(qkv, 3, axis=-1)

        def to_blocks(t):
            return t.transpose(0, 2, 1, 3).reshape(b, H, nb, BS, D).transpose(2, 0, 1, 3, 4)
        qb, kb, vb = (to_blocks(q), to_blocks(k), to_blocks(v))
        qd_ = qd[None]
        kd_ = kd[None]
        bd_ = bd[None]

        def step(state, blk):
            qi, ki, vi = blk
            aw = jnp.einsum('bhid,bhjd->bhij', qi, ki) * dd
            intra = jnp.einsum('bhij,bhjd->bhid', aw, vi)
            inter = jnp.einsum('bhid,bhde->bhie', qi * qd_, state)
            new_state = state * bd_ + jnp.einsum('bhsd,bhse->bhde', ki * kd_, vi)
            return (new_state, intra + inter)
        state0 = jnp.zeros((b, H, D, D), hidden_states.dtype)
        _, ys = jax.lax.scan(step, state0, (qb, kb, vb))
        attn = ys.transpose(1, 2, 0, 3, 4).reshape(b, H, s, D)
        attn = attn.transpose(0, 2, 1, 3).reshape(b, s, H * D)
        attn = _rmsnorm(attn, norm_w)
        gate = jax.nn.sigmoid(hidden_states @ gate_w.T)
        return gate * attn @ out_w.T

    def _L3_ffn_ref(hidden_states, router_w, w_gate, w_up, w_down, sw_gate, sw_up, sw_down, shared_gate_w):
        import jax, jax.numpy as jnp
        import numpy as np
        E = 8
        TOP_K = 2
        H = 256
        I = 176
        SI = 704
        B, S, Hd = hidden_states.shape
        x = hidden_states.reshape(-1, Hd)
        shared = jnp.einsum('ts,sh->th', jax.nn.silu(x @ sw_gate) * (x @ sw_up), sw_down)
        logits = x @ router_w.T
        probs = jax.nn.softmax(logits.astype(jnp.float32), axis=-1)
        top_w, top_i = jax.lax.top_k(probs, TOP_K)
        top_w = top_w / jnp.sum(top_w, axis=-1, keepdims=True)
        combine = jnp.sum(jax.nn.one_hot(top_i, E, dtype=x.dtype) * top_w[..., None].astype(x.dtype), axis=1)
        h = jax.nn.silu(jnp.einsum('th,ehi->eti', x, w_gate)) * jnp.einsum('th,ehi->eti', x, w_up)
        expert_out = jnp.einsum('eti,eih->eth', h, w_down)
        routed = jnp.einsum('eth,te->th', expert_out, combine)
        shared_out = jax.nn.sigmoid(x @ shared_gate_w)[:, None] * shared
        return (routed + shared_out).reshape(B, S, Hd)
    x = L0_attn_hidden_states
    xn = _layernorm(x, axis=-1)
    x = x + _L0_attn_ref(xn, L0_attn_Wq, L0_attn_Wk, L0_attn_Wv, L0_attn_conv_q, L0_attn_conv_k, L0_attn_conv_v, L0_attn_A_log, L0_attn_dt_bias, L0_attn_Wsv, L0_attn_Wb1, L0_attn_bb1, L0_attn_Wb2, L0_attn_bb2, L0_attn_Wa1, L0_attn_ba1, L0_attn_Wa2, L0_attn_ba2, L0_attn_Wg1, L0_attn_Wg2, L0_attn_bg2, L0_attn_norm_w, L0_attn_Wo) + _L0_ffn_ref(xn, L0_ffn_w1, L0_ffn_w2, L0_ffn_w3)
    xn = _layernorm(x, axis=-1)
    x = x + _L1_attn_ref(xn, L1_attn_Wq, L1_attn_Wk, L1_attn_Wv, L1_attn_Wo, L1_attn_bo) + _L1_ffn_ref(xn, L1_ffn_w_gate_up, L1_ffn_w_down)
    xn = _layernorm(x, axis=-1)
    x = x + _L2_attn_ref(xn, L2_attn_wq, L2_attn_bq, L2_attn_wk, L2_attn_bk, L2_attn_wv, L2_attn_bv, L2_attn_wo, L2_attn_bo) + _L2_ffn_ref(xn, L2_ffn_gate_weight, L2_ffn_fc_up_blocks_scale, L2_ffn_fc_up_global_scale, L2_ffn_fc_down_blocks_scale, L2_ffn_fc_down_global_scale, L2_ffn_fc_up_qweights, L2_ffn_fc_down_qweights)
    xn = _layernorm(x, axis=-1)
    x = x + _L3_attn_ref(xn, L3_attn_qkv_w, L3_attn_out_w, L3_attn_gate_w, L3_attn_norm_w) + _L3_ffn_ref(xn, L3_ffn_router_w, L3_ffn_w_gate, L3_ffn_w_up, L3_ffn_w_down, L3_ffn_sw_gate, L3_ffn_sw_up, L3_ffn_sw_down, L3_ffn_shared_gate_w)
    return x

_drawn_inputs = setup_inputs


def setup_inputs(seed=0):
    import zlib

    import numpy as np

    out = dict(_drawn_inputs(seed))
    spreads = {'L0_attn_dt_bias': (0.0, 0.8),
     'L0_attn_bb1': (0.0, 0.8),
     'L0_attn_ba1': (0.0, 0.8),
     'L0_attn_bg2': (0.0, 0.8),
     'L0_attn_norm_w': (1.0, 0.6),
     'L1_attn_bo': (0.0, 0.8),
     'L2_attn_bq': (0.0, 2.0),
     'L2_attn_bk': (0.0, 2.0),
     'L2_attn_bv': (0.0, 2.0),
     'L2_attn_bo': (0.0, 2.0),
     'L3_attn_norm_w': (1.0, 0.6)}
    factors = {'L0_attn_Wq': 8.0,
     'L0_attn_Wk': 8.0,
     'L0_attn_Wv': 8.0,
     'L0_attn_conv_q': 8.0,
     'L0_attn_conv_k': 8.0,
     'L0_attn_conv_v': 8.0,
     'L0_attn_A_log': 8.0,
     'L0_attn_Wsv': 8.0,
     'L0_attn_Wb1': 8.0,
     'L0_attn_Wb2': 8.0,
     'L0_attn_Wa1': 8.0,
     'L0_attn_Wa2': 8.0,
     'L0_attn_Wg1': 8.0,
     'L0_attn_Wg2': 8.0,
     'L0_attn_Wo': 8.0,
     'L1_attn_Wq': 8.0,
     'L1_attn_Wk': 8.0,
     'L1_attn_Wv': 8.0,
     'L1_attn_Wo': 8.0,
     'L1_ffn_w_gate_up': 8.0,
     'L1_ffn_w_down': 8.0,
     'L2_attn_wq': 29.485,
     'L2_attn_wk': 29.616,
     'L2_attn_wv': 29.161,
     'L2_attn_wo': 8.0,
     'L2_ffn_gate_weight': 8.0,
     'L2_ffn_fc_up_blocks_scale': 8.0,
     'L2_ffn_fc_down_blocks_scale': 8.0,
     'L3_attn_qkv_w': 64.0,
     'L3_attn_out_w': 36.674,
     'L3_attn_gate_w': 64.0,
     'L3_ffn_router_w': 8.0,
     'L3_ffn_w_gate': 8.0,
     'L3_ffn_w_up': 8.0,
     'L3_ffn_w_down': 8.0,
     'L3_ffn_sw_gate': 8.0,
     'L3_ffn_sw_up': 8.0,
     'L3_ffn_sw_down': 8.0,
     'L3_ffn_shared_gate_w': 8.0}
    for name, (base, spread) in spreads.items():
        noise = np.random.default_rng([zlib.crc32(name.encode()), seed]).standard_normal(out[name].shape)
        drawn = base * np.exp(spread * noise) if base else spread * noise
        out[name] = jnp.asarray(drawn.astype(out[name].dtype))
    for name, factor in factors.items():
        out[name] = (out[name] * factor).astype(out[name].dtype)
    return out
```

```python
from contextlib import ExitStack

import numpy as np
import concourse.bass as bass
from concourse import mybir

ALU = mybir.AluOpType
ACT = mybir.ActivationFunctionType
F32 = mybir.dt.float32
I32 = mybir.dt.int32
AX = mybir.AxisListType.X
ds = bass.ds

P = 128
B, S, D = 2, 1024, 256
NT = B * S // P
KD = D // P
GRP = 512
NG = B * S // GRP


class Resident:
    pass


class Chain:

    def __init__(self, eng, sem, base):
        self.eng, self.sem, self.base, self.n = eng, sem, base, 0

    def did(self, instruction):
        instruction.then_inc(self.sem, 1)
        self.n += 1
        return self.n

    def need(self, step):
        self.eng.wait_ge(self.sem, self.base + step)

    def link(self, instruction):
        self.need(self.did(instruction))


def bc(ap, axis, n):
    v = ap.unsqueeze(axis)
    shape = list(v.shape)
    shape[axis] = n
    return v.to_broadcast(shape)


def stage_semaphores(nc, c, prefix):
    held = []

    def sem(name):
        held.append(nc.alloc_semaphore(prefix + name))
        return held[-1]

    def release():
        nc.clear_and_free_semaphores(held)
        nc.all_engine_barrier()

    c.callback(release)
    return sem


def load_constants(nc, T, ins):
    with ExitStack() as c:
        sem = stage_semaphores(nc, c, "")
        x_loaded, filled = sem("x_loaded"), sem("filled")
        with nc.Block() as block:

            @block.sync
            def _(sp):
                sp.dma_start(T.x[:], ins["x"].rearrange("(t p) d -> p t d", p=P)).then_inc(x_loaded, 16)
                sp.dma_start(T.masks[:], ins["masks"]).then_inc(x_loaded, 16)
                sp.dma_start(T.ident[:], ins["ident"]).then_inc(x_loaded, 16)
                sp.wait_ge(x_loaded, 48)

            @block.gpsimd
            def _(pool):
                nc.gpsimd.memset(T.ones[:], 1.0).then_inc(filled, 1)
                nc.gpsimd.memset(T.mhalf[:], -0.5).then_inc(filled, 1)
                pool.wait_ge(filled, 2)


def layer_norm(nc, T, name):
    with ExitStack() as c:
        sb = lambda n, s: c.enter_context(nc.sbuf_tensor(name + n, s, F32))
        sem = stage_semaphores(nc, c, name)
        xn, sq = sb("xn", [P, NT, D]), sb("sq", [P, NT, D])
        mean, var, rstd = sb("mean", [P, NT]), sb("var", [P, NT]), sb("rstd", [P, NT])
        banks = c.enter_context(nc.psum_tensor(name + "ps", [P, KD * NG, GRP], F32))
        steps, squared, var_ready, rstd_ready = sem("steps"), sem("squared"), sem("varr"), sem("rstdr")
        xn_ready, transposed = sem("xnr"), sem("transposed")
        copied = sem("copied")
        with nc.Block() as block:

            @block.vector
            def _(dve):
                ch = Chain(dve, steps, 0)
                ch.link(nc.vector.tensor_reduce(mean[:], T.x[:], AX, ALU.add))
                ch.link(nc.vector.tensor_scalar(mean[:], mean[:], 1.0 / D, None, ALU.mult))
                ch.did(nc.vector.tensor_tensor(xn[:], T.x[:], bc(mean[:], 2, D), ALU.subtract))
                dve.wait_ge(squared, 1)
                ch.link(nc.vector.tensor_reduce(var[:], sq[:], AX, ALU.add))
                nc.vector.tensor_scalar(var[:], var[:], 1.0 / D, 1e-5, ALU.mult, ALU.add).then_inc(var_ready, 1)
                dve.wait_ge(rstd_ready, 1)
                nc.vector.tensor_tensor(xn[:], xn[:], bc(rstd[:], 2, D), ALU.mult).then_inc(xn_ready, 1)
                for g in range(0, KD * NG, 2):
                    dve.wait_ge(transposed, g + 1)
                    nc.vector.tensor_copy(T.xnT[:, g // NG, (g % NG) * GRP:(g % NG + 1) * GRP],
                                          banks[:, g, :]).then_inc(copied, 1)

            @block.scalar
            def _(act):
                act.wait_ge(steps, 3)
                nc.scalar.activation(sq[:], xn[:], ACT.Square).then_inc(squared, 1)
                for g in range(1, KD * NG, 2):
                    act.wait_ge(transposed, g + 1)
                    nc.scalar.activation(T.xnT[:, g // NG, (g % NG) * GRP:(g % NG + 1) * GRP],
                                         banks[:, g, :], ACT.Copy).then_inc(copied, 1)

            @block.gpsimd
            def _(pool):
                pool.wait_ge(var_ready, 1)
                nc.gpsimd.tensor_tensor(rstd[:], var[:], T.mhalf[:, 0:1].to_broadcast([P, NT]),
                                        ALU.pow).then_inc(rstd_ready, 1)

            @block.tensor
            def _(pe):
                pe.wait_ge(xn_ready, 1)
                for g in range(KD * NG):
                    for j in range(GRP // P):
                        last = nc.tensor.transpose(banks[:, g, j * P:(j + 1) * P],
                                                   xn[:, (g % NG) * 4 + j, (g // NG) * P:(g // NG + 1) * P],
                                                   T.ident[:])
                    last.then_inc(transposed, 1)


def store_output(nc, T, out):
    with nc.semaphore("stored") as stored, nc.Block() as block:

        @block.sync
        def _(sp):
            sp.dma_start(out.rearrange("(t p) d -> p t d", p=P), T.x[:]).then_inc(stored, 16)
            sp.wait_ge(stored, 16)


H0 = 16
LV = 7
NC = GRP // P
LOG1P = [0.9999998102178482, -0.4999744938483488, 0.332761765715057, -0.24499611724511947,
         0.17757023992206541, -0.10785367917046076, 0.04421419233713881, -0.008574676204512008]
TINY = 1e-10
W_Q, W_K, W_V, W_CONV, W_DT, W_A, W_BG = 0, 256, 512, 768, 780, 781, 782
W_O, W_G2, W_END = 783, 1039, 1167


def delta_attention(nc, T, ins):
    DVE_K, ACT_K, POOL_K = T.counts["l0"]
    with ExitStack() as c:
        sb = lambda n, s: c.enter_context(nc.sbuf_tensor("d_" + n, s, F32))
        sem = stage_semaphores(nc, c, "d_")
        wts = sb("wts", [P, 2, W_END])
        negA = sb("negA", [P, 2, 1])
        bgh = sb("bgh", [P, 2, 1])
        wsv = sb("wsv", [P, P])
        wg1 = sb("wg1", [P, KD, P])
        g1T = sb("g1T", [P, B * S])
        nw = sb("nw", [P, 1])
        mlp = sb("mlp", [P, 5, 64])
        mb2 = sb("mb2", [P, 2])
        powers = sb("powers", [P, 6])
        raw = sb("raw", [P, 2, 3, 3 + GRP])
        qkv = sb("qkv", [P, 2, 3, GRP])
        sq = sb("sq", [P, 2, 2, GRP])
        vtok = sb("vtok", [P, 2, GRP])
        err = sb("err", [P, 2, GRP])
        dotp = sb("dotp", [P, 2, GRP])
        junk = sb("junk", [P, 2, 3, GRP])
        tg = sb("tg", [P, 2, GRP])
        st = sb("st", [P, 2, 6, NC])
        pw = sb("pw", [P, 2, 6, NC])
        dot, l1 = sb("dot", [P, 2, NC]), sb("l1", [P, 2, NC])
        s3, t4 = sb("s3", [P, 2, NC]), sb("t4", [P, 2, NC])
        rnk = sb("rnk", [P, 2, NC])
        hid = sb("hid", [P, 2, NC, 64])
        hid2 = sb("hid2", [P, 2, NC, 64])
        ba = sb("ba", [P, 2, NC, 2])
        beta, negb = sb("beta", [P, 2, NC]), sb("negb", [P, 2, NC])
        a1 = sb("a1", [P, 2, NC])
        z = sb("z", [P, 2, GRP])
        kF = sb("kF", [P, 2, GRP])
        ez = sb("ez", [P, 2, GRP])
        mz = sb("mz", [P, 2, GRP])
        lp = sb("lp", [P, 2, GRP])
        kq = sb("kq", [P, 2, 2, GRP])
        tot = sb("tot", [P, 2, 2 * GRP])
        Aqk = sb("Aqk", [P, 2, GRP])
        MQ = sb("MQ", [P, 2, NC, 2, P])
        Xs = sb("Xs", [P, 2, GRP])
        Tm, TT = sb("Tm", [P, 2, GRP]), sb("TT", [P, 2, GRP])
        vb = sb("vb", [P, 2, GRP])
        khat, R, Dl, osq, og = dotp, mz, err, z, lp
        St = sb("St", [P, 2, P])
        ssr, rr = sb("ssr", [P, 2, NC]), sb("rr", [P, 2, NC])
        ps = c.enter_context(nc.psum_tensor("d_ps", [P, 2, 4, GRP], F32))
        tot_at = [2 * GRP - (2 * GRP >> lv) for lv in range(LV + 1)]

        rounded = sem("rounded")
        const_loaded, g1_done, g1_copied = sem("const_loaded"), sem("g1_done"), sem("g1_copied")
        powers_set = sem("powers_set")
        wts_loaded, derived, reset_done, unit_done = sem("wts"), sem("derived"), sem("reset"), sem("unit_done")
        dve_steps, act_steps, pool_steps = sem("dve_steps"), sem("act_steps"), sem("pool_steps")
        proj, evac, conv, act_qkv, squares = sem("proj"), sem("evac"), sem("conv"), sem("actqkv"), sem("squares")
        heads_mm, norms_mm = sem("heads_mm"), sem("norms_mm")
        vtok_ready, err_ready, sums_ready = sem("vtok"), sem("err"), sem("sums")
        pow_in, pow_out, s3_ready, hid_ready = sem("pow_in"), sem("pow_out"), sem("s3"), sem("hid")
        hid_silu, beta_in, beta_exp, scal_ready = sem("hid_silu"), sem("beta_in"), sem("beta_exp"), sem("scal")
        bcast_mm, z_ready, ez_ready, sp_ready, w_ready = sem("bc_mm"), sem("z"), sem("ez"), sem("sp"), sem("w")
        diag_mm, diag_copied, init_ready, vb_ready = sem("diag"), sem("diagc"), sem("init"), sem("vb")
        level_mm, masked, decayed, summed = sem("level_mm"), sem("masked"), sem("decayed"), sem("summed")
        x_mm, xs_ready, y_mm, t_ready = sem("x_mm"), sem("xs"), sem("y_mm"), sem("t")
        kh_mm, kh_ready = sem("kh_mm"), sem("kh")
        w_mm, r_ready, dl_mm, dl_ready, s_mm, s_ready = (sem("w_mm"), sem("r"), sem("dl_mm"), sem("dl"),
                                                          sem("s_mm"), sem("s"))
        osq_ready, og_ready, ss_mm, y_out_mm = sem("osq"), sem("og"), sem("ss_mm"), sem("yo_mm")
        ms_ready, rms_ready = sem("ms"), sem("rms")

        LANES = (0, 1)
        ch_ = lambda k: slice(k * P, (k + 1) * P)

        with nc.Block() as block:

            @block.sync
            def _(sp):
                for dst, src in ((wsv[:], ins["wsvT"]), (wg1[:], ins["wg1T"]), (nw[:], ins["norm_w"]),
                                 (mlp[:], ins["mlp"]), (mb2[:], ins["mb2"])):
                    sp.dma_start(dst, src).then_inc(const_loaded, 16)
                with sp.Fori(0, H0 // 2) as hp:
                    sp.wait_ge(unit_done, hp * (B * S // GRP * 2) + 2)
                    sp.dma_start(wts[:], ins["headw"][ds(hp * 2, 2)].rearrange("h p w -> p h w")).then_inc(wts_loaded, 16)

            @block.gpsimd
            def _(pool):
                for e, value in ((0, 0.5), (3, -0.5), (5, 0.5)):
                    nc.gpsimd.memset(powers[:, e:e + (3 if e == 0 else 2 if e == 3 else 1)], value).then_inc(powers_set, 1)
                pool.wait_ge(powers_set, 3)
                pool.wait_ge(const_loaded, 80)
                pool.sem_inc(unit_done, 2)
                with pool.Fori(0, H0 // 2) as hp:
                    with pool.Fori(0, B) as b:
                        bi = hp * B + b
                        with pool.Fori(0, S // GRP) as half:
                            it = bi * (S // GRP) + half
                            ch = Chain(pool, pool_steps, it * POOL_K)
                            for L in LANES:
                                n = it * 2 + L + 1
                                pool.wait_ge(pow_in, n)
                                nc.gpsimd.tensor_tensor(pw[:, L], st[:, L], bc(powers[:], 2, NC), ALU.pow).then_inc(pow_out, 1)
                            for L in LANES:
                                n = it * 2 + L + 1
                                pool.wait_ge(s3_ready, n)
                                for e, src in enumerate((pw[:, L, 0], l1[:, L], s3[:, L])):
                                    dst = hid if e == 0 else hid2
                                    ch.link(nc.gpsimd.tensor_tensor(dst[:, L], bc(src, 2, 64), bc(mlp[:, e], 1, NC), ALU.mult))
                                    if e:
                                        ch.link(nc.gpsimd.tensor_tensor(hid[:, L], hid[:, L], hid2[:, L], ALU.add))
                                nc.gpsimd.tensor_tensor(hid[:, L], hid[:, L], bc(mlp[:, 3], 1, NC), ALU.add).then_inc(hid_ready, 1)
                            for L in LANES:
                                n = it * 2 + L + 1
                                pool.wait_ge(scal_ready, n)
                                nc.gpsimd.tensor_tensor(vb[:, L].rearrange("p (c v) -> p c v", c=NC),
                                                        vtok[:, L].rearrange("p (c v) -> p c v", c=NC),
                                                        bc(beta[:, L], 2, P), ALU.mult).then_inc(vb_ready, 1)
                            for L in LANES:
                                n = it * 2 + L + 1
                                pool.wait_ge(diag_copied, n)
                                nc.gpsimd.tensor_tensor(kq[:, L, 0], kF[:, L], tot[:, L, 0:GRP], ALU.mult).then_inc(init_ready, 1)
                            for lv in range(LV):
                                h = 1 << lv
                                for L in LANES:
                                    n = it * 2 + L + 1
                                    segs = GRP // h
                                    t_l = tot[:, L, tot_at[lv]:tot_at[lv] + segs].rearrange("p (m two) -> p m two", two=2)
                                    t_n = tot[:, L, tot_at[lv + 1]:tot_at[lv + 1] + segs // 2]
                                    pool.wait_ge(level_mm, it * (2 * LV) + 2 * lv + L + 1)
                                    v = kq[:, L].rearrange("p x (m two h) -> p x m two h", two=2, h=h)
                                    f = kF[:, L].rearrange("p (m two h) -> p m two h", two=2, h=h)
                                    for x in (0, 1):
                                        ch.did(nc.gpsimd.tensor_tensor(v[:, x, :, 1], v[:, x, :, 1], bc(t_l[:, :, 0], 2, h), ALU.mult))
                                    ch.did(nc.gpsimd.tensor_tensor(f[:, :, 0], f[:, :, 0], bc(t_l[:, :, 1], 2, h), ALU.mult))
                                    k = ch.did(nc.gpsimd.tensor_tensor(t_n, t_l[:, :, 0], t_l[:, :, 1], ALU.mult))
                                    ch.need(k)
                                    pool.wait_ge(masked, it * (2 * LV) + 2 * lv + L + 1)
                                    nc.gpsimd.tensor_tensor(Aqk[:, L].rearrange("p (c i) -> p c i", c=NC),
                                                            Aqk[:, L].rearrange("p (c i) -> p c i", c=NC),
                                                            MQ[:, L, :, 1, :], ALU.add).then_inc(summed, 1)
                                    pool.wait_ge(summed, it * (2 * LV) + 2 * lv + L + 1)
                            for L in LANES:
                                n = it * 2 + L + 1
                                pool.wait_ge(ms_ready, n)
                                nc.gpsimd.tensor_tensor(rr[:, L], ssr[:, L], T.mhalf[:, 0:1].to_broadcast([P, NC]), ALU.pow).then_inc(rms_ready, 1)
                            assert ch.n == POOL_K, ("pool", ch.n)

            @block.tensor
            def _(pe):
                pe.wait_ge(const_loaded, 80)
                for g in range(NG):
                    for kd in range(KD):
                        last = nc.tensor.matmul(ps[:, 0, g, :], wg1[:, kd], T.xnT[:, kd, g * GRP:(g + 1) * GRP],
                                                start=(kd == 0), stop=(kd == KD - 1))
                    last.then_inc(g1_done, 1)
                pe.wait_ge(g1_copied, NG)
                with pe.Fori(0, H0 // 2) as hp:
                    with pe.Fori(0, B) as b:
                        with pe.Fori(0, S // GRP) as half:
                            it = (hp * B + b) * (S // GRP) + half
                            tok = (b * (S // GRP) + half) * GRP
                            for L in LANES:
                                n = it * 2 + L + 1
                                if L == 0:
                                    pe.wait_ge(wts_loaded, hp * 16 + 16)
                                    pe.wait_ge(reset_done, (hp * B + b) * 2 + 2)
                                pe.wait_ge(unit_done, n)
                                for x, w0 in enumerate((W_Q, W_K, W_V)):
                                    for kd in range(KD):
                                        last = nc.tensor.matmul(ps[:, L, x, :], wts[:, L, w0 + kd * P:w0 + (kd + 1) * P],
                                                                T.xnT[:, kd, ds(tok, GRP)], start=(kd == 0), stop=(kd == KD - 1))
                                last.then_inc(proj, 1)
                            for L in LANES:
                                n = it * 2 + L + 1
                                pe.wait_ge(rounded, n)
                                for k in range(NC):
                                    nc.tensor.transpose(ps[:, L, 0, ch_(k)], qkv[:, L, 2, ch_(k)], T.ident[:])
                                for k in range(NC):
                                    nc.tensor.matmul(ps[:, L, 1, ch_(k)], qkv[:, L, 1, ch_(k)], wsv[:], start=True, stop=True)
                                nc.tensor.matmul(ps[:, L, 2, :], wts[:, L, W_G2:W_END], g1T[:, ds(tok, GRP)],
                                                 start=True, stop=True).then_inc(heads_mm, 1)
                                pe.wait_ge(squares, n)
                                for x in (1, 0):
                                    for k in range(NC):
                                        j = (1 - x) * NC + k
                                        last = nc.tensor.matmul(ps[:, L, 3, j:j + 1], sq[:, L, x, ch_(k)], T.ones[:, 0:1], start=True, stop=True)
                                last.then_inc(norms_mm, 1)
                            for L in LANES:
                                n = it * 2 + L + 1
                                pe.wait_ge(scal_ready, n)
                                pe.wait_ge(sums_ready, n)
                                for k in range(NC):
                                    nc.tensor.matmul(ps[:, L, 0, ch_(k)], a1[:, L, k:k + 1].to_broadcast([P, P]), T.ident[:], start=True, stop=True)
                                for k in range(NC):
                                    last = nc.tensor.matmul(ps[:, L, 1, ch_(k)], pw[:, L, 3, k:k + 1].to_broadcast([P, P]), T.ident[:], start=True, stop=True)
                                last.then_inc(bcast_mm, 1)
                            for L in LANES:
                                n = it * 2 + L + 1
                                pe.wait_ge(z_ready, n)
                                for k in range(NC):
                                    last = nc.tensor.matmul(ps[:, L, 3, ch_(k)], kF[:, L, ch_(k)], qkv[:, L, 0, ch_(k)], start=True, stop=True)
                                last.then_inc(diag_mm, 1)

                            def level_products(lv):
                                for L in LANES:
                                    n = it * 2 + L + 1
                                    if lv == 0:
                                        pe.wait_ge(init_ready, n)
                                        pe.wait_ge(diag_copied, n)
                                    else:
                                        pe.wait_ge(summed, it * (2 * LV) + 2 * (lv - 1) + L + 1)
                                    for k in range(NC):
                                        last = nc.tensor.matmul(ps[:, L, k // 2, (k % 2) * 256:(k % 2 + 1) * 256].rearrange("p (x i) -> p x i", x=2), kF[:, L, ch_(k)],
                                                                kq[:, L, :, ch_(k)], start=True, stop=True)
                                    last.then_inc(level_mm, 1)

                            level_products(0)
                            for lv in range(LV):
                                for L in LANES:
                                    pe.wait_ge(masked, it * (2 * LV) + 2 * lv + L + 1)
                                    if lv:
                                        pe.wait_ge(t_ready, it * (2 * LV) + 2 * (lv - 1) + L + 1)
                                    for k in range(NC):
                                        last = nc.tensor.matmul(ps[:, L, 2, ch_(k)], MQ[:, L, k, 0, :],
                                                                Tm[:, L, ch_(k)] if lv else T.ident[:], start=True, stop=True)
                                    last.then_inc(x_mm, 1)
                                if lv + 1 < LV:
                                    level_products(lv + 1)
                                for L in LANES:
                                    pe.wait_ge(xs_ready, it * (2 * LV) + 2 * lv + L + 1)
                                    if lv == 0:
                                        for k in range(NC):
                                            last = nc.tensor.transpose(ps[:, L, 3, ch_(k)], Xs[:, L, ch_(k)], T.ident[:])
                                    else:
                                        if lv + 1 < LV:
                                            for k in range(NC):
                                                nc.tensor.matmul(ps[:, L, 3, ch_(k)], TT[:, L, ch_(k)], Xs[:, L, ch_(k)], start=True, stop=True)
                                        for k in range(NC):
                                            last = nc.tensor.matmul(ps[:, L, 2, ch_(k)], Xs[:, L, ch_(k)], TT[:, L, ch_(k)], start=True, stop=True)
                                    last.then_inc(y_mm, 1)
                            for L in LANES:
                                pe.wait_ge(summed, it * (2 * LV) + 2 * (LV - 1) + L + 1)
                                for k in range(NC):
                                    last = nc.tensor.transpose(ps[:, L, 0, ch_(k)], kF[:, L, ch_(k)], T.ident[:])
                                last.then_inc(kh_mm, 1)
                            for k in range(NC):
                                for L in LANES:
                                    n = it * 2 + L + 1
                                    if k == 0:
                                        pe.wait_ge(t_ready, it * (2 * LV) + 2 * (LV - 1) + L + 1)
                                        pe.wait_ge(kh_ready, n)
                                    else:
                                        pe.wait_ge(s_ready, it * (2 * NC) + 2 * (k - 1) + L + 1)
                                    nc.tensor.matmul(ps[:, L, 2, ch_(k)], kq[:, L, 0, ch_(k)], St[:, L], start=True, stop=True).then_inc(w_mm, 1)
                                for L in LANES:
                                    pe.wait_ge(r_ready, it * (2 * NC) + 2 * k + L + 1)
                                    nc.tensor.matmul(ps[:, L, 3, ch_(k)], TT[:, L, ch_(k)], R[:, L, ch_(k)], start=True, stop=True).then_inc(dl_mm, 1)
                                for L in LANES:
                                    nc.tensor.matmul(ps[:, L, 1, ch_(k)], St[:, L], kq[:, L, 1, ch_(k)], start=True, stop=False)
                                    pe.wait_ge(dl_ready, it * (2 * NC) + 2 * k + L + 1)
                                    nc.tensor.matmul(ps[:, L, 1, ch_(k)], Dl[:, L, ch_(k)], Aqk[:, L, ch_(k)], start=False, stop=True)
                                    nc.tensor.matmul(ps[:, L, 0, 0:P], khat[:, L, ch_(k)], Dl[:, L, ch_(k)], start=True, stop=True).then_inc(s_mm, 1)
                            for L in LANES:
                                n = it * 2 + L + 1
                                pe.wait_ge(osq_ready, n)
                                for k in range(NC):
                                    last = nc.tensor.matmul(ps[:, L, 3, k:k + 1], osq[:, L, ch_(k)], T.ones[:, 0:1], start=True, stop=True)
                                last.then_inc(ss_mm, 1)
                                pe.wait_ge(og_ready, n)
                                for k in range(NC):
                                    last = nc.tensor.matmul(ps[:, L, k // 2, (k % 2) * D:(k % 2 + 1) * D], og[:, L, ch_(k)],
                                                            wts[:, L, W_O:W_G2], start=True, stop=True)
                                last.then_inc(y_out_mm, 1)

            @block.scalar
            def _(act):
                for g in range(NG):
                    act.wait_ge(g1_done, g + 1)
                    nc.scalar.activation(g1T[:, g * GRP:(g + 1) * GRP], ps[:, 0, g, :], ACT.Copy).then_inc(g1_copied, 1)
                with act.Fori(0, H0 // 2) as hp:
                    act.wait_ge(wts_loaded, hp * 16 + 16)
                    nc.scalar.activation(negA[:], wts[:, :, W_A:W_A + 1], ACT.Exp).then_inc(derived, 1)
                    act.wait_ge(derived, hp * 3 + 1)
                    nc.scalar.mul(negA[:], negA[:], -1.0).then_inc(derived, 1)
                    nc.scalar.mul(bgh[:], wts[:, :, W_BG:W_BG + 1], 0.5).then_inc(derived, 1)
                    act.wait_ge(derived, hp * 3 + 3)
                    with act.Fori(0, B) as b:
                        act.wait_ge(reset_done, (hp * B + b) * 2 + 2)
                        with act.Fori(0, S // GRP) as half:
                            it = (hp * B + b) * (S // GRP) + half
                            ch = Chain(act, act_steps, it * ACT_K)
                            for L in LANES:
                                n = it * 2 + L + 1
                                act.wait_ge(proj, n)
                                ch.link(nc.scalar.activation(raw[:, L, :, 0:3], raw[:, L, :, GRP:GRP + 3], ACT.Copy))
                                for x in range(3):
                                    nc.scalar.activation(qkv[:, L, x], ps[:, L, x, :], ACT.Copy,
                                                         scale=wts[:, L, W_CONV + x * 4 + 3:W_CONV + x * 4 + 4])
                                for x in range(3):
                                    last = nc.scalar.activation(raw[:, L, x, 3:3 + GRP], ps[:, L, x, :], ACT.Copy)
                                last.then_inc(evac, 1)
                            for L in LANES:
                                n = it * 2 + L + 1
                                act.wait_ge(conv, 3 * n)
                                nc.scalar.activation(qkv[:, L], qkv[:, L], ACT.Silu).then_inc(act_qkv, 1)
                            for L in LANES:
                                n = it * 2 + L + 1
                                act.wait_ge(rounded, n)
                                nc.scalar.activation(sq[:, L], qkv[:, L, 0:2], ACT.Square).then_inc(squares, 1)
                            for L in LANES:
                                n = it * 2 + L + 1
                                act.wait_ge(heads_mm, n)
                                nc.scalar.activation(vtok[:, L], ps[:, L, 0, :], ACT.Copy).then_inc(vtok_ready, 1)
                                nc.scalar.activation(tg[:, L], ps[:, L, 2, :], ACT.Tanh, bias=bgh[:, L], scale=0.5)
                            for L in LANES:
                                n = it * 2 + L + 1
                                act.wait_ge(err_ready, n)
                                act.wait_ge(vtok_ready, n)
                                for e, src in ((2, vtok[:, L]), (0, err[:, L]), (1, ps[:, L, 1, :])):
                                    for k in range(NC):
                                        last = nc.scalar.activation(junk[:, L, e, ch_(k)], src[:, ch_(k)], ACT.Square,
                                                                    accum_out=st[:, L, e, k:k + 1])
                                last.then_inc(sums_ready, 1)
                            for L in LANES:
                                n = it * 2 + L + 1
                                act.wait_ge(hid_ready, n)
                                nc.scalar.activation(hid[:, L], hid[:, L], ACT.Silu).then_inc(hid_silu, 1)
                            for L in LANES:
                                n = it * 2 + L + 1
                                act.wait_ge(beta_in, n)
                                nc.scalar.activation(beta[:, L], ba[:, L, :, 0], ACT.Exp, scale=-1.0).then_inc(beta_exp, 1)
                            for L in LANES:
                                n = it * 2 + L + 1
                                act.wait_ge(z_ready, n)
                                ch.link(nc.scalar.activation(ez[:, L], z[:, L], ACT.Abs, bias=wts[:, L, W_DT:W_DT + 1]))
                                nc.scalar.activation(ez[:, L], ez[:, L], ACT.Exp, scale=-1.0).then_inc(ez_ready, 1)
                            for L in LANES:
                                n = it * 2 + L + 1
                                act.wait_ge(sp_ready, n)
                                nc.scalar.activation(tot[:, L, 0:GRP], lp[:, L], ACT.Exp, scale=negA[:, L]).then_inc(w_ready, 1)
                            for lv in range(LV):
                                for L in LANES:
                                    act.wait_ge(x_mm, it * (2 * LV) + 2 * lv + L + 1)
                                    for k in range(NC):
                                        last = nc.scalar.activation(Xs[:, L, ch_(k)], ps[:, L, 2, ch_(k)], ACT.Copy, scale=beta[:, L, k:k + 1])
                                    last.then_inc(xs_ready, 1)
                            for L in LANES:
                                n = it * 2 + L + 1
                                act.wait_ge(kh_mm, n)
                                nc.scalar.activation(khat[:, L], ps[:, L, 0, :], ACT.Copy).then_inc(kh_ready, 1)
                            for k in range(NC):
                                for L in LANES:
                                    act.wait_ge(dl_mm, it * (2 * NC) + 2 * k + L + 1)
                                    nc.scalar.activation(Dl[:, L, ch_(k)], ps[:, L, 3, ch_(k)], ACT.Copy).then_inc(dl_ready, 1)
                            for L in LANES:
                                act.wait_ge(s_mm, it * (2 * NC) + 2 * (NC - 1) + L + 1)
                                nc.scalar.activation(osq[:, L], ps[:, L, 1, :], ACT.Square).then_inc(osq_ready, 1)
                            assert ch.n == ACT_K, ("act", ch.n)

            @block.vector
            def _(dve):
                with dve.Fori(0, H0 // 2) as hp:
                    with dve.Fori(0, B) as b:
                        dve.wait_ge(unit_done, (hp * B + b) * (S // GRP * 2) + 2)
                        nc.vector.memset(St[:], 0.0).then_inc(reset_done, 1)
                        nc.vector.memset(raw[:, :, :, GRP:GRP + 3], 0.0).then_inc(reset_done, 1)
                        with dve.Fori(0, S // GRP) as half:
                            it = (hp * B + b) * (S // GRP) + half
                            ch = Chain(dve, dve_steps, it * DVE_K)
                            for L in LANES:
                                n = it * 2 + L + 1
                                if L == 0:
                                    dve.wait_ge(wts_loaded, hp * 16 + 16)
                                    dve.wait_ge(reset_done, (hp * B + b) * 2 + 2)
                                dve.wait_ge(evac, n)
                                for i in range(3):
                                    for x in range(3):
                                        if i:
                                            ch.need(ch.n - (2 if i == 1 else 2 - x))
                                        tap = nc.vector.scalar_tensor_tensor(
                                            qkv[:, L, x], raw[:, L, x, i:i + GRP], wts[:, L, W_CONV + x * 4 + i:W_CONV + x * 4 + i + 1],
                                            qkv[:, L, x], ALU.mult, ALU.add)
                                        if i < 2:
                                            ch.did(tap)
                                        else:
                                            tap.then_inc(conv, 1)
                            for L in LANES:
                                n = it * 2 + L + 1
                                dve.wait_ge(act_qkv, n)
                                nc.vector.tensor_scalar(qkv[:, L], qkv[:, L], TINY, -TINY, ALU.add, ALU.add).then_inc(rounded, 1)
                            for L in LANES:
                                n = it * 2 + L + 1
                                dve.wait_ge(vtok_ready, n)
                                ch.did(nc.vector.tensor_tensor(err[:, L], ps[:, L, 1, :], vtok[:, L], ALU.subtract))
                                nc.vector.tensor_tensor(dotp[:, L], ps[:, L, 1, :], vtok[:, L], ALU.mult).then_inc(err_ready, 1)
                                dve.wait_ge(err_ready, n)
                                ch.did(nc.vector.tensor_reduce(dot[:, L], dotp[:, L].rearrange("p (c v) -> p c v", c=NC), AX, ALU.add))
                                ch.did(nc.vector.tensor_reduce(l1[:, L], err[:, L].rearrange("p (c v) -> p c v", c=NC), AX, ALU.add, apply_absolute_value=True))
                                dve.wait_ge(norms_mm, n)
                                ch.did(nc.vector.tensor_scalar(st[:, L, 3:5], ps[:, L, 3, 0:2 * NC].rearrange("p (a c) -> p a c", a=2), 1e-6, None, ALU.add))
                                ch.did(nc.vector.tensor_copy(st[:, L, 5], ps[:, L, 3, 0:NC]))
                            for L in LANES:
                                n = it * 2 + L + 1
                                dve.wait_ge(sums_ready, n)
                                nc.vector.tensor_scalar(st[:, L, 0:3], st[:, L, 0:3], 1e-6, None, ALU.add).then_inc(pow_in, 1)
                            for L in LANES:
                                n = it * 2 + L + 1
                                dve.wait_ge(pow_out, n)
                                ch.link(nc.vector.tensor_tensor(t4[:, L], pw[:, L, 1], pw[:, L, 2], ALU.mult))
                                ch.link(nc.vector.tensor_scalar(t4[:, L], t4[:, L], 1e-6, None, ALU.add))
                                ch.link(nc.vector.reciprocal(t4[:, L], t4[:, L]))
                                ch.link(nc.vector.tensor_tensor(t4[:, L], t4[:, L], dot[:, L], ALU.mult))
                                nc.vector.tensor_scalar(s3[:, L], t4[:, L], -1.0, 1.0, ALU.mult, ALU.add).then_inc(s3_ready, 1)
                                ch.link(nc.vector.tensor_scalar(rnk[:, L], pw[:, L, 5], 1e-12, None, ALU.max))
                                ch.link(nc.vector.reciprocal(rnk[:, L], rnk[:, L]))
                            for L in LANES:
                                n = it * 2 + L + 1
                                dve.wait_ge(hid_silu, n)
                                ch.link(nc.vector.tensor_tensor(hid2[:, L], hid[:, L], bc(mlp[:, 4], 1, NC), ALU.mult))
                                ch.link(nc.vector.tensor_reduce(ba[:, L], hid2[:, L].rearrange("p c (m j) -> p c m j", m=2), AX, ALU.add))
                                ch.link(nc.vector.tensor_tensor(ba[:, L], ba[:, L], bc(mb2[:], 1, NC), ALU.add))
                                nc.vector.tensor_scalar(ba[:, L, :, 0], ba[:, L, :, 0], -87.0, None, ALU.max).then_inc(beta_in, 1)
                            for L in LANES:
                                n = it * 2 + L + 1
                                dve.wait_ge(beta_in, n)
                                ch.did(nc.vector.tensor_tensor(a1[:, L], ba[:, L, :, 1], rnk[:, L], ALU.mult))
                                dve.wait_ge(beta_exp, n)
                                ch.link(nc.vector.tensor_scalar(beta[:, L], beta[:, L], 1.0, None, ALU.add))
                                ch.link(nc.vector.reciprocal(beta[:, L], beta[:, L]))
                                nc.vector.tensor_scalar(negb[:, L], beta[:, L], -1.0, None, ALU.mult).then_inc(scal_ready, 1)
                            for L in LANES:
                                n = it * 2 + L + 1
                                dve.wait_ge(bcast_mm, n)
                                k = ch.did(nc.vector.tensor_tensor(z[:, L], qkv[:, L, 1], ps[:, L, 0, :], ALU.mult))
                                nc.vector.tensor_tensor(kF[:, L], qkv[:, L, 1], ps[:, L, 1, :], ALU.mult).then_inc(z_ready, 1)
                                ch.need(k)
                                ch.did(nc.vector.tensor_scalar(mz[:, L], z[:, L], wts[:, L, W_DT:W_DT + 1], 0.0, ALU.add, ALU.max))
                            for L in LANES:
                                n = it * 2 + L + 1
                                dve.wait_ge(ez_ready, n)
                                ch.link(nc.vector.tensor_scalar(lp[:, L], ez[:, L], LOG1P[7], None, ALU.mult))
                                for i in range(6, -1, -1):
                                    ch.link(nc.vector.scalar_tensor_tensor(lp[:, L], lp[:, L], LOG1P[i], ez[:, L], ALU.add, ALU.mult))
                                nc.vector.tensor_tensor(lp[:, L], lp[:, L], mz[:, L], ALU.add).then_inc(sp_ready, 1)
                            for L in LANES:
                                n = it * 2 + L + 1
                                dve.wait_ge(diag_mm, n)
                                ch.did(nc.vector.tensor_tensor(Aqk[:, L].rearrange("p (c i) -> p c i", c=NC),
                                                               ps[:, L, 3, :].rearrange("p (c i) -> p c i", c=NC),
                                                               bc(T.ident[:], 1, NC), ALU.mult))
                                dve.wait_ge(w_ready, n)
                                ch.link(nc.vector.tensor_scalar(tot[:, L, 0:GRP], tot[:, L, 0:GRP], TINY, -TINY, ALU.add, ALU.add))
                                nc.vector.tensor_tensor(kq[:, L, 1], qkv[:, L, 0], tot[:, L, 0:GRP], ALU.mult).then_inc(diag_copied, 1)

                            def mask_level(lv):
                                for L in LANES:
                                    m = it * (2 * LV) + 2 * lv + L + 1
                                    dve.wait_ge(level_mm, m)
                                    if lv:
                                        dve.wait_ge(summed, m - 2)
                                        dve.wait_ge(x_mm, m - 2)
                                    nc.vector.scalar_tensor_tensor(MQ[:, L].rearrange("p c x i -> p (c x) i"),
                                                                   ps[:, L, 0:2, :].rearrange("p k (y i) -> p (k y) i", i=P), TINY,
                                                                   bc(T.masks[:, lv], 1, 2 * NC), ALU.add, ALU.mult).then_inc(masked, 1)

                            mask_level(0)
                            for lv in range(LV):
                                if lv + 1 < LV:
                                    mask_level(lv + 1)
                                for L in LANES:
                                    m = it * (2 * LV) + 2 * lv + L + 1
                                    dve.wait_ge(y_mm, m)
                                    c3 = lambda t: t[:, L].rearrange("p (c i) -> p c i", c=NC)
                                    if lv == 0:
                                        ch.did(nc.vector.tensor_tensor(c3(Tm), bc(T.ident[:], 1, NC), c3(Xs), ALU.subtract))
                                        nc.vector.tensor_tensor(c3(TT), bc(T.ident[:], 1, NC),
                                                                ps[:, L, 3, :].rearrange("p (c i) -> p c i", c=NC), ALU.subtract).then_inc(t_ready, 1)
                                    else:
                                        dve.wait_ge(t_ready, m - 2)
                                        if lv + 1 < LV:
                                            ch.did(nc.vector.tensor_tensor(Tm[:, L], Tm[:, L], ps[:, L, 3, :], ALU.subtract))
                                        nc.vector.tensor_tensor(TT[:, L], TT[:, L], ps[:, L, 2, :], ALU.subtract).then_inc(t_ready, 1)
                            for L in LANES:
                                n = it * 2 + L + 1
                                dve.wait_ge(vb_ready, n)
                                dve.wait_ge(kh_ready, n)
                                kg = ch.did(nc.vector.tensor_scalar(tg[:, L], tg[:, L], 0.5, 0.5, ALU.mult, ALU.add))
                            for k in range(NC):
                                for L in LANES:
                                    m = it * (2 * NC) + 2 * k + L + 1
                                    dve.wait_ge(w_mm, m)
                                    nc.vector.scalar_tensor_tensor(R[:, L, ch_(k)], ps[:, L, 2, ch_(k)], negb[:, L, k:k + 1],
                                                                   vb[:, L, ch_(k)], ALU.mult, ALU.add).then_inc(r_ready, 1)
                                for L in LANES:
                                    m = it * (2 * NC) + 2 * k + L + 1
                                    dve.wait_ge(s_mm, m)
                                    nc.vector.scalar_tensor_tensor(St[:, L], St[:, L], tot[:, L, tot_at[LV] + k:tot_at[LV] + k + 1],
                                                                   ps[:, L, 0, 0:P], ALU.mult, ALU.add).then_inc(s_ready, 1)
                                    dve.wait_ge(s_ready, m)
                            for L in LANES:
                                n = it * 2 + L + 1
                                dve.wait_ge(osq_ready, n)
                                ch.need(kg)
                                nc.vector.scalar_tensor_tensor(og[:, L], ps[:, L, 1, :], nw[:], tg[:, L], ALU.mult, ALU.mult).then_inc(og_ready, 1)
                            for L in LANES:
                                n = it * 2 + L + 1
                                dve.wait_ge(ss_mm, n)
                                ch.link(nc.vector.tensor_tensor(ssr[:, L], ps[:, L, 3, 0:NC], pw[:, L, 4], ALU.mult))
                                ch.link(nc.vector.tensor_tensor(ssr[:, L], ssr[:, L], pw[:, L, 4], ALU.mult))
                                nc.vector.tensor_scalar(ssr[:, L], ssr[:, L], 1.0 / (P * P), 1e-5, ALU.mult, ALU.add).then_inc(ms_ready, 1)
                            for L in LANES:
                                n = it * 2 + L + 1
                                dve.wait_ge(rms_ready, n)
                                ch.link(nc.vector.scalar_tensor_tensor(rr[:, L], rr[:, L], float(P) ** -0.5, pw[:, L, 4], ALU.mult, ALU.mult))
                                dve.wait_ge(y_out_mm, n)
                                for k in range(NC):
                                    tile = (b * (S // GRP) + half) * NC + k
                                    xt = T.x[:, ds(tile, 1), :].rearrange("p a d -> p (a d)")
                                    last = nc.vector.scalar_tensor_tensor(xt, ps[:, L, k // 2, (k % 2) * D:(k % 2 + 1) * D],
                                                                          rr[:, L, k:k + 1], xt, ALU.mult, ALU.add)
                                last.then_inc(unit_done, 1)
                                dve.wait_ge(unit_done, n + 2)
                            assert ch.n == DVE_K, ("dve", ch.n)


def feed_forward(nc, T, name, blocks, tiles, kind, w1, w2, wide2=True, weights=None, quant=None, scales=None):
    F = sum(n for _, n in tiles)
    NTL = len(tiles)
    parts = 1 if kind == "relu2" else 2
    with ExitStack() as c:
        sb = lambda n, s: c.enter_context(nc.sbuf_tensor(name + n, s, F32))
        sem = stage_semaphores(nc, c, name)
        w1s = sb("w1s", [P, parts, KD, F])
        w2s = sb("w2s", [P, NTL, D])
        raws = None
        if scales is not None:
            raws = (c.enter_context(nc.sbuf_tensor(name + "q1", [P, KD, F], I32)), sb("s1", [P, KD, F]),
                    c.enter_context(nc.sbuf_tensor(name + "q2", [P, D], I32)), sb("s2", [P, D]), sb("gs", [P, 2]))
        act1 = sb("act1", [P, 2, GRP])
        hid = sb("hid", [P, NTL, GRP])
        pg = c.enter_context(nc.psum_tensor(name + "pg", [P, 2, 2, GRP], F32))
        py = c.enter_context(nc.psum_tensor(name + "py", [P, 2, 2, GRP], F32))
        loaded, prepared, steps, freed = sem("loaded"), sem("prepared"), sem("steps"), sem("freed")
        up_mm, act_ready, hid_ready, y_mm, added = sem("up_mm"), sem("act"), sem("hid_r"), sem("y_mm"), sem("added")
        g_loaded = sem("g_loaded")
        n_dma = 4 if scales is not None else 2
        with nc.Block() as block:

            @block.sync
            def _(sp):
                if scales is not None:
                    sp.dma_start(raws[4][:], scales[4]).then_inc(g_loaded, 16)
                with sp.Fori(0, blocks) as e:
                    sp.wait_ge(freed, e + 1)
                    if scales is not None:
                        for dst, src in zip(raws[:4], scales[:4]):
                            flat = src[ds(e, 1)].rearrange("a p f -> p (a f)")
                            if len(dst.shape) == 3:
                                flat = flat.rearrange("p (k f) -> p k f", k=KD)
                            sp.dma_start(dst[:], flat).then_inc(loaded, 16)
                    else:
                        sp.dma_start(w1s[:].rearrange("p a k f -> p (a k f)"), w1[ds(e, 1)].rearrange("a p f -> p (a f)")).then_inc(loaded, 16)
                        sp.dma_start(w2s[:].rearrange("p t d -> p (t d)"), w2[ds(e, 1)].rearrange("a p f -> p (a f)")).then_inc(loaded, 16)

            @block.tensor
            def _(pe):
                pe.sem_inc(freed, 1)
                with pe.Fori(0, blocks) as e:
                    with pe.Fori(0, NG) as g:
                        it = e * NG + g
                        pe.wait_ge(prepared, e + 1)
                        for t, (f0, fn) in enumerate(tiles):
                            if t != 1:
                                pe.wait_ge(hid_ready, it * NTL + max(0, t - 1))
                            for a in range(parts):
                                for kd in range(KD):
                                    last = nc.tensor.matmul(pg[0:fn, t % 2, a, :], w1s[:, a, kd, f0:f0 + fn],
                                                            T.xnT[:, kd, ds(g * GRP, GRP)], start=(kd == 0), stop=(kd == KD - 1))
                            last.then_inc(up_mm, 1)
                        pe.wait_ge(hid_ready, it * NTL + NTL)
                        pe.wait_ge(added, it)
                        for k in range(4):
                            for t, (f0, fn) in enumerate(tiles):
                                last = nc.tensor.matmul(py[:, 0, k // 2, (k % 2) * D:(k % 2 + 1) * D], hid[0:fn, t, k * P:(k + 1) * P],
                                                        w2s[0:fn, t, :], start=(t == 0), stop=(t == NTL - 1))
                        last.then_inc(y_mm, 1)
                    pe.wait_ge(y_mm, e * NG + NG)
                    pe.sem_inc(freed, 1)

            @block.scalar
            def _(act):
                func = {"sigmoid": ACT.Sigmoid, "silu": ACT.Silu, "relu2": ACT.Relu}[kind]
                with act.Fori(0, blocks) as e:
                    with act.Fori(0, NG) as g:
                        it = e * NG + g
                        for t, (f0, fn) in enumerate(tiles):
                            act.wait_ge(up_mm, it * NTL + t + 1)
                            act.wait_ge(hid_ready, it * NTL + max(0, t - 1))
                            nc.scalar.activation(act1[0:fn, t % 2, :], pg[0:fn, t % 2, 0, :], func).then_inc(act_ready, 1)

            @block.vector
            def _(dve):
                if scales is not None:
                    dve.wait_ge(g_loaded, 16)
                with dve.Fori(0, blocks) as e:
                    ch = Chain(dve, steps, e * T.counts[name])
                    dve.wait_ge(loaded, e * (16 * n_dma) + 16 * n_dma)
                    if quant:
                        quant(ch, w1s, w2s, raws)
                    dve.sem_inc(prepared, 1)
                    with dve.Fori(0, NG) as g:
                        it = e * NG + g
                        for t, (f0, fn) in enumerate(tiles):
                            dve.wait_ge(act_ready, it * NTL + t + 1)
                            if t == 0:
                                dve.wait_ge(y_mm, it)
                            second = act1[0:fn, t % 2, :] if kind == "relu2" else pg[0:fn, t % 2, 1, :]
                            nc.vector.tensor_tensor(hid[0:fn, t, :], act1[0:fn, t % 2, :], second, ALU.mult).then_inc(hid_ready, 1)
                        dve.wait_ge(y_mm, it + 1)
                        dve.wait_ge(added, it)
                        for k in range(4):
                            xt = T.x[:, ds(g * 4 + k, 1), :].rearrange("p a d -> p (a d)")
                            yk = py[:, 0, k // 2, (k % 2) * D:(k % 2 + 1) * D]
                            if weights is None:
                                last = nc.vector.tensor_tensor(xt, yk, xt, ALU.add)
                            else:
                                sc = weights[:, ds(g * 4 + k, 1), ds(e, 1)].rearrange("p a b -> p (a b)")
                                last = nc.vector.scalar_tensor_tensor(xt, yk, sc, xt, ALU.mult, ALU.add)
                        last.then_inc(added, 1)
                    if quant:
                        assert ch.n == T.counts[name], (name, ch.n)


H1, KV1 = 16, 4
QT = S // P


def causal_attention(nc, T, ins):
    with ExitStack() as c:
        sb = lambda n, s: c.enter_context(nc.sbuf_tensor("c_" + n, s, F32))
        sem = stage_semaphores(nc, c, "c_")
        wq = sb("wq", [P, 2, KD, P])
        wo = sb("wo", [P, 2, D])
        wk, wv = sb("wk", [P, KD, P]), sb("wv", [P, KD, P])
        mask = sb("mask", [P, P])
        bias = sb("bias", [P, D])
        kT, vt = sb("kT", [P, S]), sb("vt", [P, QT, P])
        qT = sb("qT", [P, S])
        nmax, rsum, rinv = sb("nmax", [P, 2]), sb("rsum", [P, 2]), sb("rinv", [P, 2])
        pr = sb("pr", [P, 2, S])
        pT = sb("pT", [P, 2, S])
        oT = sb("oT", [P, 2, P])
        sc = c.enter_context(nc.psum_tensor("c_sc", [P, 2, 2, GRP], F32))
        tp = c.enter_context(nc.psum_tensor("c_tp", [P, 2, GRP], F32))
        po = c.enter_context(nc.psum_tensor("c_po", [P, GRP], F32))
        py = c.enter_context(nc.psum_tensor("c_py", [P, GRP], F32))
        consts, w_loaded, kvw_loaded = sem("consts"), sem("w_loaded"), sem("kvw")
        biased, kv_mm, kv_ready, q_mm, q_ready = sem("biased"), sem("kv_mm"), sem("kv_ready"), sem("q_mm"), sem("q_ready")
        sc_mm, diag, maxed, expd, tp_mm, tp_ready = sem("sc_mm"), sem("diag"), sem("maxed"), sem("expd"), sem("tp_mm"), sem("tp_ready")
        o_mm, o_ready, y_mm, added, rec = sem("o_mm"), sem("o_ready"), sem("y_mm"), sem("added"), sem("rec")
        NKV = 4
        TPS = [(t // 4) + 1 for t in range(QT)]
        TPT = sum(TPS)
        with nc.Block() as block:

            @block.sync
            def _(sp):
                sp.dma_start(mask[:], ins["causal"]).then_inc(consts, 16)
                sp.dma_start(bias[:], ins["bo1"]).then_inc(consts, 16)
                with sp.Fori(0, B) as b:
                    with sp.Fori(0, KV1) as kv:
                        s = b * KV1 + kv
                        sp.wait_ge(kv_mm, s * NKV)
                        sp.dma_start(wk[:], ins["wk1"][ds(kv, 1)].rearrange("a p k m -> p (a k) m")).then_inc(kvw_loaded, 16)
                        sp.dma_start(wv[:], ins["wv1"][ds(kv, 1)].rearrange("a p k m -> p (a k) m")).then_inc(kvw_loaded, 16)
                        with sp.Fori(0, H1 // KV1 // 2) as u:
                            hp = s * 2 + u
                            sp.wait_ge(y_mm, hp * (2 * QT))
                            sp.dma_start(wq[:], ins["wq1"][ds(kv * 4 + u * 2, 2)].rearrange("h p k m -> p h k m")).then_inc(w_loaded, 16)
                            sp.dma_start(wo[:], ins["wo1"][ds(kv * 4 + u * 2, 2)].rearrange("h p d -> p h d")).then_inc(w_loaded, 16)

            @block.tensor
            def _(pe):
                for b in range(B):
                    with pe.Fori(0, KV1) as kv:
                        s = b * KV1 + kv
                        pe.wait_ge(kvw_loaded, s * 32 + 32)
                        pe.wait_ge(added, s * (4 * QT))
                        for g in range(2):
                            pe.wait_ge(kv_ready, s * NKV)
                            for kd in range(KD):
                                last = nc.tensor.matmul(tp[:, g, :], wk[:, kd], T.xnT[:, kd, b * S + g * GRP:b * S + (g + 1) * GRP], start=(kd == 0), stop=(kd == KD - 1))
                            last.then_inc(kv_mm, 1)
                        for g in range(2):
                            pe.wait_ge(kv_ready, s * NKV + g + 1)
                            for t in range(4):
                                for kd in range(KD):
                                    last = nc.tensor.matmul(tp[:, g, t * P:(t + 1) * P], T.xnT[:, kd, b * S + g * GRP + t * P:b * S + g * GRP + (t + 1) * P], wv[:, kd],
                                                            start=(kd == 0), stop=(kd == KD - 1))
                            last.then_inc(kv_mm, 1)
                        with pe.Fori(0, 2) as u:
                            pe.wait_ge(kv_ready, s * NKV + NKV)
                            for w in range(2):
                                hh = s * 4 + u * 2 + w
                                if w == 0:
                                    pe.wait_ge(w_loaded, (s * 2 + u) * 32 + 32)
                                pe.wait_ge(tp_ready, hh * TPT)
                                pe.wait_ge(q_ready, hh * 2)
                                for g in range(2):
                                    for kd in range(KD):
                                        last = nc.tensor.matmul(tp[:, g, :], wq[:, w, kd], T.xnT[:, kd, b * S + g * GRP:b * S + (g + 1) * GRP], start=(kd == 0), stop=(kd == KD - 1))
                                    last.then_inc(q_mm, 1)
                                pe.wait_ge(q_ready, hh * 2 + 2)

                                def scores(t):
                                    pe.wait_ge(expd, hh * QT + max(0, t - 1))
                                    for k in range(t // 4 + 1):
                                        n = min(GRP, (t + 1) * P - k * GRP)
                                        last = nc.tensor.matmul(sc[:, t % 2, k, 0:n], qT[:, t * P:(t + 1) * P], kT[:, k * GRP:k * GRP + n], start=True, stop=True)
                                    last.then_inc(sc_mm, 1)

                                def project(t):
                                    pe.wait_ge(o_ready, hh * QT + t + 1)
                                    pe.wait_ge(added, hh * QT + t)
                                    nc.tensor.matmul(py[:, 0:D], oT[:, t % 2, :], wo[:, w, :], start=True, stop=True).then_inc(y_mm, 1)

                                scores(0)
                                scores(1)
                                for t in range(QT):
                                    pe.wait_ge(expd, hh * QT + t + 1)
                                    for k in range(TPS[t]):
                                        done = sum(TPS[:t]) + k
                                        if done >= 2:
                                            pe.wait_ge(tp_ready, hh * TPT + done - 1)
                                        for j in range(min(4, t + 1 - 4 * k)):
                                            last = nc.tensor.transpose(tp[:, done % 2, j * P:(j + 1) * P], pr[:, t % 2, (4 * k + j) * P:(4 * k + j + 1) * P], T.ident[:])
                                        last.then_inc(tp_mm, 1)
                                    if t + 2 < QT:
                                        scores(t + 2)
                                    if t:
                                        project(t - 1)
                                    pe.wait_ge(tp_ready, hh * TPT + sum(TPS[:t + 1]))
                                    pe.wait_ge(o_ready, hh * QT + t)
                                    for j in range(t + 1):
                                        last = nc.tensor.matmul(po[:, 0:P], vt[:, j, :], pT[:, t % 2, j * P:(j + 1) * P], start=(j == 0), stop=(j == t))
                                    last.then_inc(o_mm, 1)
                                project(QT - 1)

            @block.scalar
            def _(act):
                with act.Fori(0, B) as b:
                    with act.Fori(0, KV1) as kv:
                        s = b * KV1 + kv
                        for g in range(2):
                            act.wait_ge(kv_mm, s * NKV + g + 1)
                            nc.scalar.activation(kT[:, g * GRP:(g + 1) * GRP], tp[:, g, :], ACT.Copy).then_inc(kv_ready, 1)
                        for g in range(2):
                            act.wait_ge(kv_mm, s * NKV + 2 + g + 1)
                            nc.scalar.activation(vt[:, 4 * g:4 * g + 4, :].rearrange("p t d -> p (t d)"), tp[:, g, :], ACT.Copy).then_inc(kv_ready, 1)
                        with act.Fori(0, 2) as u:
                            for w in range(2):
                                hh = s * 4 + u * 2 + w
                                for g in range(2):
                                    act.wait_ge(q_mm, hh * 2 + g + 1)
                                    nc.scalar.activation(qT[:, g * GRP:(g + 1) * GRP], tp[:, g, :], ACT.Copy).then_inc(q_ready, 1)

                                def probs(t):
                                    act.wait_ge(maxed, hh * QT + t + 1)
                                    act.wait_ge(tp_mm, hh * TPT + sum(TPS[:max(0, t - 1)]))
                                    act.wait_ge(rec, hh * QT + max(0, t - 1))
                                    n = (t + 1) * P
                                    nc.scalar.activation(pr[:, t % 2, 0:n], sc[:, t % 2].rearrange("p k n -> p (k n)")[:, 0:n], ACT.Exp, bias=nmax[:, t % 2:t % 2 + 1],
                                                         accum_out=rsum[:, t % 2:t % 2 + 1]).then_inc(expd, 1)

                                probs(0)
                                for t in range(QT):
                                    for k in range(TPS[t]):
                                        done = sum(TPS[:t]) + k
                                        act.wait_ge(tp_mm, hh * TPT + done + 1)
                                        n = P * min(4, t + 1 - 4 * k)
                                        nc.scalar.activation(pT[:, t % 2, k * GRP:k * GRP + n], tp[:, done % 2, 0:n], ACT.Copy).then_inc(tp_ready, 1)
                                    if t + 1 < QT:
                                        probs(t + 1)
                                    act.wait_ge(o_mm, hh * QT + t + 1)
                                    nc.scalar.activation(oT[:, t % 2, :], po[:, 0:P], ACT.Copy).then_inc(o_ready, 1)

            @block.vector
            def _(dve):
                dve.wait_ge(consts, 32)
                nc.vector.tensor_tensor(T.x[:], T.x[:], bc(bias[:], 1, NT), ALU.add).then_inc(biased, 1)
                dve.wait_ge(biased, 1)
                with dve.Fori(0, B) as b:
                    with dve.Fori(0, KV1 * 2) as s2:
                        for w in range(2):
                            hh = (b * (KV1 * 2) + s2) * 2 + w

                            def row_max(t):
                                dve.wait_ge(sc_mm, hh * QT + t + 1)
                                d0 = (t % 4) * P
                                nc.vector.tensor_tensor(sc[:, t % 2, t // 4, d0:d0 + P], sc[:, t % 2, t // 4, d0:d0 + P], mask[:], ALU.add).then_inc(diag, 1)
                                dve.wait_ge(diag, hh * QT + t + 1)
                                nc.vector.tensor_reduce(nmax[:, t % 2:t % 2 + 1], sc[:, t % 2].rearrange("p k n -> p (k n)")[:, 0:(t + 1) * P], AX, ALU.max, negate=True).then_inc(maxed, 1)

                            row_max(0)
                            row_max(1)
                            for t in range(QT):
                                if t + 2 < QT:
                                    row_max(t + 2)
                                dve.wait_ge(expd, hh * QT + t + 1)
                                nc.vector.reciprocal(rinv[:, t % 2:t % 2 + 1], rsum[:, t % 2:t % 2 + 1]).then_inc(rec, 1)
                                dve.wait_ge(rec, hh * QT + t + 1)
                                dve.wait_ge(y_mm, hh * QT + t + 1)
                                dve.wait_ge(added, hh * QT + t)
                                xt = T.x[:, ds(b * QT + t, 1), :].rearrange("p a d -> p (a d)")
                                nc.vector.scalar_tensor_tensor(xt, py[:, 0:D], rinv[:, t % 2:t % 2 + 1], xt, ALU.mult, ALU.add).then_inc(added, 1)


H2, G2, D2 = 16, 2, 16
PAD = 32


def rotary_attention(nc, T, ins):
    with ExitStack() as c:
        sb = lambda n, s: c.enter_context(nc.sbuf_tensor("r_" + n, s, F32))
        sem = stage_semaphores(nc, c, "r_")
        W = D + 2 * G2 * D2
        wqkv = sb("wqkv", [P, KD, W])
        bqkv = sb("bqkv", [P, W])
        wo, bo = sb("wo", [P, KD, D]), sb("bo", [P, D])
        cos, sin = sb("cos", [P, QT, D2]), sb("sin", [P, QT, D2])
        NR = H2 + G2
        lin = sb("lin", [P, W])
        rc, rs = sb("rc", [P, NR, D2]), sb("rs", [P, NR, D2])
        qp = sb("qp", [P, H2, PAD])
        kp = sb("kp", [P, G2, 4, PAD])
        qT = sb("qT", [P, 4, B * S])
        kT = sb("kT", [P, G2, B * S])
        v1 = sb("v1", [P, NT, G2, D2 + 1])
        nmax, rinv = sb("nmax", [P, 2]), sb("rinv", [P, 1])
        pr, pT = sb("pr", [P, 2, S]), sb("pT", [P, 2, S])
        oall = sb("oall", [P, H2, D2])
        oT = sb("oT", [P, KD, P])
        xt_s = sb("xt_s", [P, KD, P])
        qt_s = sb("qt_s", [P, 4, P])
        sc = c.enter_context(nc.psum_tensor("r_sc", [P, 2, 2, GRP], F32))
        tp = c.enter_context(nc.psum_tensor("r_tp", [P, 2, GRP], F32))
        po = c.enter_context(nc.psum_tensor("r_po", [P, GRP], F32))
        py = c.enter_context(nc.psum_tensor("r_py", [P, GRP], F32))
        names = ("staged qstaged loaded zeroed steps lin_mm padded t_mm t_copied sc_mm maxed expd tp_mm tp_ready o_mm o_ready oT_mm oT_ready y_mm added").split()
        (staged, qstaged, loaded, zeroed, steps, lin_mm, padded, t_mm, t_copied, sc_mm, maxed, expd, tp_mm, tp_ready, o_mm, o_ready, oT_mm,
         oT_ready, y_mm, added) = [sem(n) for n in names]
        with nc.Block() as block:

            @block.sync
            def _(sp):
                for dst, name in ((wqkv, "w2qkv"), (bqkv, "b2qkv"), (wo, "w2o"), (bo, "b2o"), (cos, "cos"), (sin, "sin")):
                    sp.dma_start(dst[:], ins[name]).then_inc(loaded, 16)

            @block.gpsimd
            def _(pool):
                nc.gpsimd.memset(qp[:], 0.0).then_inc(zeroed, 1)
                nc.gpsimd.memset(kp[:], 0.0).then_inc(zeroed, 1)
                nc.gpsimd.memset(v1[:], 1.0).then_inc(zeroed, 1)

            @block.tensor
            def _(pe):
                pe.wait_ge(loaded, 96)
                with pe.Fori(0, NT) as t:
                    pe.wait_ge(steps, t * STEPS2)
                    pe.wait_ge(staged, t + 1)
                    for kd in range(KD):
                        last = nc.tensor.matmul(po[:, 0:W], xt_s[:, kd], wqkv[:, kd], start=(kd == 0), stop=(kd == KD - 1))
                    last.then_inc(lin_mm, 1)
                    pe.wait_ge(padded, t + 1)
                    pe.wait_ge(t_copied, t * 2)
                    for j in range(4):
                        last = nc.tensor.transpose(tp[:, 0, j * P:(j + 1) * P], qp[:, 4 * j:4 * j + 4].rearrange("p h d -> p (h d)"), T.ident[:])
                    for g in range(G2):
                        last = nc.tensor.transpose(tp[:, 1, g * P:(g + 1) * P], kp[:, g].rearrange("p h d -> p (h d)"), T.ident[:])
                    last.then_inc(t_mm, 1)
                pe.wait_ge(t_copied, NT * 2)
                for b in range(B):
                    with pe.Fori(0, QT) as tq:
                        t = b * QT + tq
                        pe.wait_ge(qstaged, t + 1)
                        for h in range(H2):
                            def scores(h):
                                pe.wait_ge(expd, t * H2 + max(0, h - 1))
                                r = slice((h % 4) * PAD, (h % 4 + 1) * PAD)
                                b0 = slice(b * S, b * S + GRP), slice(b * S + GRP, (b + 1) * S)
                                for k in range(2):
                                    last = nc.tensor.matmul(sc[:, h % 2, k, :], qt_s[r, h // 4, :], kT[r, h // (H2 // G2), b0[k]], start=True, stop=True,
                                                            tile_position=((h % 4) * PAD, 0))
                                last.then_inc(sc_mm, 1)

                            def output(h):
                                pe.wait_ge(tp_ready, (t * H2 + h) * 2 + 2)
                                pe.wait_ge(o_ready, t * H2 + h)
                                for j in range(QT):
                                    last = nc.tensor.matmul(po[:, 0:D2 + 1], pT[:, h % 2, j * P:(j + 1) * P],
                                                            v1[:, b * QT + j, h // (H2 // G2), :], start=(j == 0), stop=(j == QT - 1))
                                last.then_inc(o_mm, 1)

                            if h == 0:
                                scores(0)
                                scores(1)
                            pe.wait_ge(expd, t * H2 + h + 1)
                            for k in range(2):
                                pe.wait_ge(tp_ready, (t * H2 + h) * 2)
                                for j in range(4):
                                    last = nc.tensor.transpose(tp[:, k, j * P:(j + 1) * P], pr[:, h % 2, (4 * k + j) * P:(4 * k + j + 1) * P], T.ident[:])
                                last.then_inc(tp_mm, 1)
                            if h + 2 < H2:
                                scores(h + 2)
                            if h:
                                output(h - 1)
                        output(H2 - 1)
                        pe.wait_ge(o_ready, t * H2 + H2)
                        for kd in range(KD):
                            last = nc.tensor.transpose(po[:, kd * P:(kd + 1) * P], oall[:].rearrange("p h d -> p (h d)")[:, kd * P:(kd + 1) * P], T.ident[:])
                        last.then_inc(oT_mm, 1)
                        pe.wait_ge(oT_ready, t + 1)
                        pe.wait_ge(added, t)
                        for kd in range(KD):
                            last = nc.tensor.matmul(py[:, 0:D], oT[:, kd], wo[:, kd], start=(kd == 0), stop=(kd == KD - 1))
                        last.then_inc(y_mm, 1)

            @block.scalar
            def _(act):
                with act.Fori(0, NT) as t:
                    act.wait_ge(lin_mm, t)
                    nc.scalar.activation(xt_s[:], T.xnT[:, :, ds(t * P, P)], ACT.Copy).then_inc(staged, 1)
                    act.wait_ge(t_mm, t + 1)
                    nc.scalar.activation(qT[:, :, ds(t * P, P)], tp[:, 0, :].rearrange("p (j i) -> p j i", j=4), ACT.Copy).then_inc(t_copied, 1)
                    nc.scalar.activation(kT[:, :, ds(t * P, P)], tp[:, 1, 0:2 * P].rearrange("p (j i) -> p j i", j=2), ACT.Copy).then_inc(t_copied, 1)
                with act.Fori(0, NT) as t:
                    act.wait_ge(t_copied, 2 * NT)
                    act.wait_ge(sc_mm, t * H2)
                    nc.scalar.activation(qt_s[:], qT[:, :, ds(t * P, P)], ACT.Copy, scale=1.0 / D2).then_inc(qstaged, 1)

                    def probs(h):
                        act.wait_ge(maxed, t * H2 + h + 1)
                        act.wait_ge(tp_mm, (t * H2 + max(0, h - 1)) * 2)
                        nc.scalar.activation(pr[:, h % 2], sc[:, h % 2].rearrange("p k n -> p (k n)"), ACT.Exp, bias=nmax[:, h % 2:h % 2 + 1]).then_inc(expd, 1)
                    for h in range(H2):
                        if h == 0:
                            probs(0)
                        for k in range(2):
                            act.wait_ge(tp_mm, (t * H2 + h) * 2 + k + 1)
                            nc.scalar.activation(pT[:, h % 2, k * GRP:(k + 1) * GRP], tp[:, k, :], ACT.Copy).then_inc(tp_ready, 1)
                        if h + 1 < H2:
                            probs(h + 1)
                    act.wait_ge(oT_mm, t + 1)
                    nc.scalar.activation(oT[:].rearrange("p k i -> p (k i)"), po[:, 0:KD * P], ACT.Copy).then_inc(oT_ready, 1)

            @block.vector
            def _(dve):
                dve.wait_ge(loaded, 96)
                dve.wait_ge(zeroed, 3)
                with dve.Fori(0, NT) as t:
                    ch = Chain(dve, steps, t * STEPS2)
                    dve.wait_ge(lin_mm, t + 1)
                    dve.wait_ge(t_mm, t)
                    ch.link(nc.vector.tensor_tensor(lin[:], po[:, 0:W], bqkv[:], ALU.add))
                    qk = lin[:, 0:NR * D2].rearrange("p (h d) -> p h d", d=D2)
                    ct = cos[:, ds(t % QT, 1), :].to_broadcast([P, NR, D2])
                    sn = lambda a, b: sin[:, ds(t % QT, 1), a:b].to_broadcast([P, NR, D2 // 2])
                    ch.did(nc.vector.tensor_tensor(rc[:], qk, ct, ALU.mult))
                    ch.did(nc.vector.tensor_tensor(rs[:, :, 0:8], qk[:, :, 8:16], sn(0, 8), ALU.mult))
                    ch.link(nc.vector.tensor_tensor(rs[:, :, 8:16], qk[:, :, 0:8], sn(8, 16), ALU.mult))
                    ch.did(nc.vector.tensor_tensor(qp[:, :, 0:D2], rc[:, 0:H2], rs[:, 0:H2], ALU.add))
                    for g in range(G2):
                        ch.did(nc.vector.tensor_tensor(kp[:, g, :, 0:D2], rc[:, H2 + g:H2 + g + 1].to_broadcast([P, 4, D2]),
                                                       rs[:, H2 + g:H2 + g + 1].to_broadcast([P, 4, D2]), ALU.add))
                    nc.vector.tensor_copy(v1[:, ds(t, 1), :, 0:D2].rearrange("p a g d -> p (a g) d"),
                                          lin[:, NR * D2:W].rearrange("p (g d) -> p g d", g=G2)).then_inc(padded, 1)
                    dve.wait_ge(padded, t + 1)
                    assert ch.n == STEPS2, ch.n
                nc.vector.tensor_tensor(T.x[:], T.x[:], bc(bo[:], 1, NT), ALU.add).then_inc(steps, 1)
                dve.wait_ge(steps, NT * STEPS2 + 1)
                with dve.Fori(0, NT) as t:
                    ch = Chain(dve, steps, NT * STEPS2 + 1 + t * H2)
                    def row_max(h):
                        dve.wait_ge(sc_mm, t * H2 + h + 1)
                        dve.wait_ge(expd, t * H2 + max(0, h - 1))
                        nc.vector.tensor_reduce(nmax[:, h % 2:h % 2 + 1], sc[:, h % 2].rearrange("p k n -> p (k n)"), AX, ALU.max, negate=True).then_inc(maxed, 1)
                    for h in range(H2):
                        if h == 0:
                            row_max(0)
                            row_max(1)
                        if h + 2 < H2:
                            row_max(h + 2)
                        dve.wait_ge(o_mm, t * H2 + h + 1)
                        ch.link(nc.vector.reciprocal(rinv[:], po[:, D2:D2 + 1]))
                        nc.vector.tensor_scalar(oall[:, h], po[:, 0:D2], rinv[:], None, ALU.mult).then_inc(o_ready, 1)
                        dve.wait_ge(o_ready, t * H2 + h + 1)
                    dve.wait_ge(y_mm, t + 1)
                    xt = T.x[:, ds(t, 1), :].rearrange("p a d -> p (a d)")
                    nc.vector.tensor_tensor(xt, py[:, 0:D], xt, ALU.add).then_inc(added, 1)


STEPS2 = 7


def route(nc, T, name, E, w, weights, log_sigmoid, shared=None):
    cols = E + (shared is not None)
    with ExitStack() as c:
        sb = lambda n, s: c.enter_context(nc.sbuf_tensor(name + n, s, F32))
        sem = stage_semaphores(nc, c, name)
        ws = sb("w", [P, KD, cols])
        order = sb("order", [P, E])
        lg, e1, p, key, sel, both = [sb(n, [P, NT, E]) for n in ("lg", "e1", "p", "key", "sel", "both")]
        m, tot = sb("m", [P, NT]), sb("tot", [P, NT])
        zs = sb("zs", [P, NT])
        ps = c.enter_context(nc.psum_tensor(name + "ps", [P, NT, cols], F32))
        loaded, steps, mm, asked, answered = sem("loaded"), sem("steps"), sem("mm"), sem("asked"), sem("answered")
        with nc.Block() as block:

            @block.sync
            def _(sp):
                sp.dma_start(ws[:], w).then_inc(loaded, 16)
                sp.dma_start(order[:], T.ins["order"][:, 16 - E:16]).then_inc(loaded, 16)

            @block.tensor
            def _(pe):
                pe.wait_ge(loaded, 32)
                for t in range(NT):
                    for kd in range(KD):
                        last = nc.tensor.matmul(ps[:, t, :], T.xnT[:, kd, t * P:(t + 1) * P], ws[:, kd], start=(kd == 0), stop=(kd == KD - 1))
                last.then_inc(mm, 1)

            @block.scalar
            def _(act):
                if log_sigmoid:
                    act.wait_ge(asked, 1)
                    nc.scalar.activation(e1[:], lg[:], ACT.Abs).then_inc(answered, 1)
                    act.wait_ge(answered, 1)
                    nc.scalar.activation(e1[:], e1[:], ACT.Exp, scale=-1.0).then_inc(answered, 1)
                    act.wait_ge(answered, 2)
                    nc.scalar.activation(e1[:], e1[:], ACT.Ln, bias=T.ones[:, 0:1]).then_inc(answered, 1)
                act.wait_ge(asked, 1 + log_sigmoid)
                nc.scalar.activation(p[:], p[:], ACT.Exp).then_inc(answered, 1)
                if shared is not None:
                    for copy in range(2):
                        nc.scalar.activation(shared[:, :, copy], zs[:], ACT.Sigmoid).then_inc(answered, 1)

            @block.vector
            def _(dve):
                ch = Chain(dve, steps, 0)
                TTS = lambda o, a, b, op: ch.link(nc.vector.tensor_tensor(o, a, b, op))
                dve.wait_ge(loaded, 32)
                dve.wait_ge(mm, 1)
                if log_sigmoid:
                    nc.vector.tensor_copy(lg[:], ps[:, :, 0:E]).then_inc(asked, 1)
                else:
                    ch.link(nc.vector.tensor_copy(lg[:], ps[:, :, 0:E]))
                if shared is not None:
                    ch.link(nc.vector.tensor_copy(zs[:], ps[:, :, E]))
                if log_sigmoid:
                    dve.wait_ge(answered, 3)
                    ch.link(nc.vector.tensor_scalar(lg[:], lg[:], 0.0, None, ALU.min))
                    TTS(lg[:], lg[:], e1[:], ALU.subtract)
                ch.link(nc.vector.tensor_reduce(m[:], lg[:], AX, ALU.max))
                nc.vector.tensor_tensor(p[:], lg[:], bc(m[:], 2, E), ALU.subtract).then_inc(asked, 1)
                dve.wait_ge(answered, 1 + 3 * log_sigmoid)
                ch.link(nc.vector.tensor_reduce(tot[:], p[:], AX, ALU.add))
                ch.link(nc.vector.reciprocal(tot[:], tot[:]))
                TTS(p[:], p[:], bc(tot[:], 2, E), ALU.mult)
                ch.link(nc.vector.tensor_copy(e1[:], p[:]))
                for best in range(2):
                    ch.link(nc.vector.tensor_reduce(m[:], e1[:], AX, ALU.max))
                    TTS(key[:], e1[:], bc(m[:], 2, E), ALU.is_equal)
                    TTS(key[:], key[:], bc(order[:], 1, NT), ALU.mult)
                    ch.link(nc.vector.tensor_reduce(m[:], key[:], AX, ALU.max))
                    TTS(sel[:], key[:], bc(m[:], 2, E), ALU.is_equal)
                    if best == 0:
                        ch.link(nc.vector.tensor_copy(both[:], sel[:]))
                        ch.link(nc.vector.tensor_scalar(sel[:], sel[:], 2.0, None, ALU.mult))
                        TTS(e1[:], e1[:], sel[:], ALU.subtract)
                    else:
                        TTS(both[:], both[:], sel[:], ALU.add)
                TTS(p[:], p[:], both[:], ALU.mult)
                ch.link(nc.vector.tensor_reduce(tot[:], p[:], AX, ALU.add))
                if log_sigmoid:
                    ch.link(nc.vector.tensor_scalar(tot[:], tot[:], 1e-20, None, ALU.add))
                ch.link(nc.vector.reciprocal(tot[:], tot[:]))
                TTS(weights[:], p[:], bc(tot[:], 2, E), ALU.mult)


H3, D3 = 32, 64


def decay_attention(nc, T, ins):
    with ExitStack() as c:
        sb = lambda n, s: c.enter_context(nc.sbuf_tensor("e_" + n, s, F32))
        sem = stage_semaphores(nc, c, "e_")
        wqk = sb("wqk", [P, 3, KD, P])
        wkv = sb("wkv", [P, KD, 2 * P])
        wo = sb("wo", [P, D])
        nw = sb("nw", [P, 1])
        dec = sb("dec", [P, 2, P])
        qd = sb("qd", [P, P])
        kd_ = sb("kd", [P, 2 * D3])
        cd = sb("cd", [P, 1])
        qkT, gT = sb("qkT", [P, 2, GRP]), sb("gT", [P, GRP])
        qT, kT = qkT[:, 0], qkT[:, 1]
        qdT = sb("qdT", [P, GRP])
        xg = sb("xg", [P, KD, GRP])
        kv = sb("kv", [P, 4, 2 * P])
        kvd = sb("kvd", [P, 4, P])
        at = sb("at", [P, 4, 2, P])
        St = sb("St", [P, 2 * D3])
        osq, og = sb("osq", [P, GRP]), sb("og", [P, GRP])
        yacc, ssacc, rms = sb("yacc", [P, NT, D]), sb("ssacc", [P, NT]), sb("rms", [P, NT])
        ps = c.enter_context(nc.psum_tensor("e_ps", [P, 8, GRP], F32))
        names = ("kd_rounded rounded staged zeroed loaded reset unit qkg_mm qkg kv_mm kvr scale steps at_mm at_r o_mm s_mm s_r osq og ss_mm y_mm fin rmsr").split()
        (kd_rounded, rounded, staged, zeroed, loaded, reset, unit_done, qkg_mm, qkg_ready, kv_mm, kv_ready, scaled, steps, at_mm, at_ready, o_mm, s_mm,
         s_ready, osq_ready, og_ready, ss_mm, y_mm, fin, rms_ready) = [sem(n) for n in names]
        halves = S // GRP
        with nc.Block() as block:

            @block.sync
            def _(sp):
                with sp.Fori(0, H3 // 2) as hp:
                    sp.wait_ge(unit_done, hp * (B * halves))
                    for dst, name in ((wqk[:].rearrange("p a k m -> p (a k m)"), "w3qk"), (wkv[:].rearrange("p k m -> p (k m)"), "w3kv"),
                                      (wo[:], "w3o"), (dec[:].rearrange("p a i -> p (a i)"), "w3dec"), (qd[:], "w3qd"),
                                      (kd_[:], "w3kd"), (cd[:], "w3cd"), (nw[:], "w3nw")):
                        sp.dma_start(dst, ins[name][ds(hp, 1)].rearrange("a p f -> p (a f)")).then_inc(loaded, 16)

            @block.gpsimd
            def _(pool):
                nc.gpsimd.memset(yacc[:], 0.0).then_inc(zeroed, 1)
                nc.gpsimd.memset(ssacc[:], 0.0).then_inc(zeroed, 1)
                with pool.Fori(0, H3 // 2) as hp:
                    with pool.Fori(0, B) as b:
                        with pool.Fori(0, halves) as half:
                            it = (hp * B + b) * halves + half
                            pool.wait_ge(unit_done, it)
                            for kd in range(KD):
                                nc.gpsimd.tensor_copy(xg[:, kd], T.xnT[:, kd, ds((b * halves + half) * GRP, GRP)]).then_inc(staged, 1)
                            pool.wait_ge(loaded, hp * 128 + 128)
                            pool.wait_ge(rounded, it * 2 + 1)
                            nc.gpsimd.tensor_tensor(qdT[:].rearrange("p (c i) -> p c i", c=4), qT.rearrange("p (c i) -> p c i", c=4),
                                                    bc(qd[:], 1, 4), ALU.mult).then_inc(scaled, 1)
                            pool.wait_ge(rounded, it * 2 + 2)
                            nc.gpsimd.tensor_tensor(kvd[:], kv[:, :, 0:P], bc(kd_[:], 1, 4), ALU.mult).then_inc(scaled, 1)
                pool.wait_ge(fin, 1)
                nc.gpsimd.tensor_tensor(rms[:], ssacc[:], T.mhalf[:, 0:1].to_broadcast([P, NT]), ALU.pow).then_inc(rms_ready, 1)

            @block.tensor
            def _(pe):
                with pe.Fori(0, H3 // 2) as hp:
                    with pe.Fori(0, B) as b:
                        with pe.Fori(0, halves) as half:
                            it = (hp * B + b) * halves + half
                            tok = (b * halves + half) * GRP
                            pe.wait_ge(loaded, hp * 128 + 128)
                            pe.wait_ge(reset, hp * B + b + 1)
                            pe.wait_ge(unit_done, it)
                            for x in range(3):
                                for kd in range(KD):
                                    last = nc.tensor.matmul(ps[:, x, :], wqk[:, x, kd], T.xnT[:, kd, ds(tok, GRP)], start=(kd == 0), stop=(kd == KD - 1))
                                last.then_inc(qkg_mm, 1)
                            pe.wait_ge(staged, it * KD + KD)
                            for g in range(2):
                                for j in range(2):
                                    for kd in range(KD):
                                        last = nc.tensor.matmul(ps[:, 3 + g, j * 2 * P:(j + 1) * 2 * P], xg[:, kd, (2 * g + j) * P:(2 * g + j + 1) * P], wkv[:, kd],
                                                                start=(kd == 0), stop=(kd == KD - 1))
                                last.then_inc(kv_mm, 1)
                            pe.wait_ge(rounded, it * 2 + 1)
                            for a in range(2):
                                for k in range(4):
                                        last = nc.tensor.matmul(ps[:, a, k * P:(k + 1) * P], kT[a * D3:(a + 1) * D3, k * P:(k + 1) * P],
                                                                qT[a * D3:(a + 1) * D3, k * P:(k + 1) * P], start=True, stop=True)
                                last.then_inc(at_mm, 1)
                            pe.wait_ge(at_ready, it * 2 + 2)
                            pe.wait_ge(kd_rounded, it + 1)
                            for k in range(4):
                                if k:
                                    pe.wait_ge(s_ready, it * 4 + k)
                                for a in range(2):
                                    r = slice(a * D3, (a + 1) * D3)
                                    nc.tensor.matmul(ps[r, 5, k * P:(k + 1) * P], kv[:, k, P + a * D3:P + (a + 1) * D3], at[:, k, a, :], start=True, stop=False)
                                nc.tensor.matmul(ps[:, 5, k * P:(k + 1) * P], St[:], qdT[:, k * P:(k + 1) * P], start=False, stop=True)
                                nc.tensor.matmul(ps[:, 6, 0:P], kvd[:, k, :], kv[:, k, P:2 * P], start=True, stop=True).then_inc(s_mm, 1)
                            pe.wait_ge(osq_ready, it + 1)
                            for k in range(4):
                                last = nc.tensor.matmul(ps[:, 7, k:k + 1], osq[:, k * P:(k + 1) * P], T.ones[:, 0:1], start=True, stop=True)
                            last.then_inc(ss_mm, 1)
                            pe.wait_ge(og_ready, it + 1)
                            for k in range(4):
                                last = nc.tensor.matmul(ps[:, 3 + k // 2, (k % 2) * D:(k % 2 + 1) * D], og[:, k * P:(k + 1) * P], wo[:], start=True, stop=True)
                            last.then_inc(y_mm, 1)

            @block.scalar
            def _(act):
                with act.Fori(0, H3 // 2 * B * halves) as it:
                    for x, (dst, func) in enumerate(((qT, ACT.Silu), (kT, ACT.Silu), (gT[:], ACT.Tanh))):
                        act.wait_ge(qkg_mm, it * 3 + x + 1)
                        nc.scalar.activation(dst, ps[:, x, :], func, scale=0.5 if x == 2 else 1.0).then_inc(qkg_ready, 1)
                    for g in range(2):
                        act.wait_ge(kv_mm, it * 2 + g + 1)
                        nc.scalar.activation(kv[:, 2 * g:2 * g + 2, :].rearrange("p j m -> p (j m)"), ps[:, 3 + g, :], ACT.Silu).then_inc(kv_ready, 1)
                    act.wait_ge(s_mm, it * 4 + 4)
                    nc.scalar.activation(osq[:], ps[:, 5, :], ACT.Square).then_inc(osq_ready, 1)

            @block.vector
            def _(dve):
                dve.wait_ge(zeroed, 2)
                with dve.Fori(0, H3 // 2) as hp:
                    with dve.Fori(0, B) as b:
                        dve.wait_ge(unit_done, (hp * B + b) * halves)
                        nc.vector.memset(St[:], 0.0).then_inc(reset, 1)
                        with dve.Fori(0, halves) as half:
                            it = (hp * B + b) * halves + half
                            dve.wait_ge(loaded, hp * 128 + 128)
                            dve.wait_ge(reset, hp * B + b + 1)
                            dve.wait_ge(qkg_ready, it * 3 + 3)
                            nc.vector.tensor_scalar(qkT[:], qkT[:], TINY, -TINY, ALU.add, ALU.add).then_inc(rounded, 1)
                            nc.vector.tensor_scalar(gT[:], gT[:], 0.5, 0.5, ALU.mult, ALU.add).then_inc(steps, 1)
                            dve.wait_ge(kv_ready, it * 2 + 2)
                            nc.vector.tensor_scalar(kv[:], kv[:], TINY, -TINY, ALU.add, ALU.add).then_inc(rounded, 1)
                            for g in range(2):
                                dve.wait_ge(at_mm, it * 2 + g + 1)
                                nc.vector.tensor_tensor(at[:, :, g], ps[:, g, :].rearrange("p (k i) -> p k i", k=4), bc(dec[:, g], 1, 4),
                                                        ALU.mult).then_inc(at_ready, 1)
                            dve.wait_ge(scaled, it * 2 + 2)
                            nc.vector.tensor_scalar(kvd[:], kvd[:], TINY, -TINY, ALU.add, ALU.add).then_inc(kd_rounded, 1)
                            for k in range(4):
                                dve.wait_ge(s_mm, it * 4 + k + 1)
                                for a in range(2):
                                    r = slice(a * D3, (a + 1) * D3)
                                    last = nc.vector.scalar_tensor_tensor(St[r, r], St[r, r], cd[r], ps[r, 6, r], ALU.mult, ALU.add)
                                last.then_inc(s_ready, 1)
                                dve.wait_ge(s_ready, it * 4 + k + 1)
                            dve.wait_ge(osq_ready, it + 1)
                            dve.wait_ge(steps, it * 3 + 1)
                            nc.vector.scalar_tensor_tensor(og[:], ps[:, 5, :], nw[:], gT[:], ALU.mult, ALU.mult).then_inc(og_ready, 1)
                            dve.wait_ge(ss_mm, it + 1)
                            sst = ssacc[:, ds((b * halves + half) * 4, 4)]
                            nc.vector.tensor_tensor(sst, sst, ps[:, 7, 0:4], ALU.add).then_inc(steps, 1)
                            dve.wait_ge(y_mm, it + 1)
                            yt = yacc[:, ds((b * halves + half) * 4, 4), :].rearrange("p (g t) d -> p g (t d)", g=2)
                            nc.vector.tensor_tensor(yt, yt, ps[:, 3:5, :], ALU.add).then_inc(steps, 1)
                            dve.wait_ge(steps, it * 3 + 3)
                            dve.sem_inc(unit_done, 1)
                nc.vector.tensor_scalar(ssacc[:], ssacc[:], 1.0 / (H3 * D3), 1e-5, ALU.mult, ALU.add).then_inc(fin, 1)
                dve.wait_ge(rms_ready, 1)
                nc.vector.tensor_tensor(yacc[:], yacc[:], bc(rms[:], 2, D), ALU.mult).then_inc(fin, 1)
                dve.wait_ge(fin, 2)
                nc.vector.tensor_tensor(T.x[:], T.x[:], yacc[:], ALU.add).then_inc(fin, 1)


def build_program(nc, ins, out, stages):
    with ExitStack() as c:
        sb = lambda n, s: c.enter_context(nc.sbuf_tensor(n, s, F32))
        T = Resident()
        T.x, T.xnT = sb("x_res", [P, NT, D]), sb("xnT", [P, KD, B * S])
        T.ident, T.ones, T.mhalf, T.masks = sb("ident", [P, P]), sb("ones", [P, P]), sb("mhalf", [P, 1]), sb("masks", [P, LV, P])
        T.ins = ins
        T.ternary = sb("ternary", [P, 3])
        T.w2, T.w3, T.shared = sb("w2", [P, NT, E2]), sb("w3", [P, NT, E3]), sb("shared", [P, NT, 2])
        T.counts = {"l0": (90, 4, 66), "f0": 9, "f1": 0, "f2": 6, "f3": 0, "fs": 0}
        load_constants(nc, T, ins)
        for name, stage in STAGES:
            if name in stages:
                stage(nc, T, ins)
        store_output(nc, T, out)


E2, E3 = 16, 8
WIDE = [(0, 128), (128, 128), (256, 96)]
MAGIC = 1.5 * 2.0 ** 23


def ternary_scales(nc, T, ins):
    with ExitStack() as c:
        sem = stage_semaphores(nc, c, "t_")
        w = c.enter_context(nc.sbuf_tensor("t_w", [P, 3, KD * 704], F32))
        sums = c.enter_context(nc.sbuf_tensor("t_sums", [P, 3], F32))
        ps = c.enter_context(nc.psum_tensor("t_ps", [P, 3], F32))
        loaded, summed, mm, steps = sem("loaded"), sem("summed"), sem("mm"), sem("steps")
        with nc.Block() as block:

            @block.sync
            def _(sp):
                sp.dma_start(w[:], ins["w0all"]).then_inc(loaded, 16)

            @block.vector
            def _(dve):
                ch = Chain(dve, steps, 0)
                dve.wait_ge(loaded, 16)
                nc.vector.tensor_reduce(sums[:], w[:], AX, ALU.add, apply_absolute_value=True).then_inc(summed, 1)
                dve.wait_ge(mm, 1)
                ch.link(nc.vector.tensor_scalar(T.ternary[:], ps[:], 1.0 / (704 * D), 1e-8, ALU.mult, ALU.add))
                ch.link(nc.vector.reciprocal(T.ternary[:], T.ternary[:]))

            @block.tensor
            def _(pe):
                pe.wait_ge(summed, 1)
                nc.tensor.matmul(ps[:], T.ones[:], sums[:], start=True, stop=True).then_inc(mm, 1)


def ffn0(nc, T, ins):
    def quantise(ch, w1, w2, raws):
        for a, w in ((0, w1[:, 0]), (1, w1[:, 1]), (2, w2[:])):
            ch.link(nc.vector.tensor_scalar(w, w, T.ternary[:, a:a + 1], MAGIC, ALU.mult, ALU.add))
            ch.link(nc.vector.tensor_scalar(w, w, -MAGIC, 1.0, ALU.add, ALU.min))
            ch.link(nc.vector.tensor_scalar(w, w, -1.0, None, ALU.max))

    feed_forward(nc, T, "f0", 2, WIDE, "sigmoid", ins["f0w1"], ins["f0w2"], quant=quantise)


def ffn2(nc, T, ins):
    def dequantise(ch, w1, w2, raws):
        q1, s1, q2, s2, gs = raws
        for a, (w, q, s) in enumerate(((w1[:, 0], q1[:], s1[:]), (w2[:, 0], q2[:], s2[:]))):
            ch.link(nc.vector.tensor_scalar(w, q, -8.0, None, ALU.add))
            ch.link(nc.vector.tensor_tensor(w, w, s, ALU.mult))
            ch.link(nc.vector.tensor_scalar(w, w, gs[:, a:a + 1], None, ALU.mult))

    feed_forward(nc, T, "f2", E2, [(0, P)], "relu2", None, None, weights=T.w2, quant=dequantise,
                 scales=[ins[n] for n in ("q1", "s1", "q2", "s2", "gs")])


STAGES = [
    ("ln0", lambda nc, T, i: layer_norm(nc, T, "n0")),
    ("l0a", delta_attention),
    ("ter", ternary_scales),
    ("l0f", ffn0),
    ("ln1", lambda nc, T, i: layer_norm(nc, T, "n1")),
    ("l1a", causal_attention),
    ("l1f", lambda nc, T, i: feed_forward(nc, T, "f1", 4, [(0, P), (P, P)], "silu", i["f1w1"], i["f1w2"])),
    ("ln2", lambda nc, T, i: layer_norm(nc, T, "n2")),
    ("l2a", rotary_attention),
    ("l2r", lambda nc, T, i: route(nc, T, "g2", E2, i["gate2"], T.w2, 1)),
    ("l2f", ffn2),
    ("ln3", lambda nc, T, i: layer_norm(nc, T, "n3")),
    ("l3a", decay_attention),
    ("l3r", lambda nc, T, i: route(nc, T, "g3", E3, i["gate3"], T.w3, 0, T.shared)),
    ("l3s", lambda nc, T, i: feed_forward(nc, T, "fs", 2, WIDE, "silu", i["fsw1"], i["fsw2"], weights=T.shared)),
    ("l3f", lambda nc, T, i: feed_forward(nc, T, "f3", E3, [(0, P), (P, 48)], "silu", i["f3w1"], i["f3w2"], weights=T.w3)),
]
RUN = [n for n, _ in STAGES]


def transposed(w):
    return np.ascontiguousarray(w.T.reshape(KD, P, -1).transpose(1, 0, 2))


def layout(v):
    f = {}
    f["x"] = v["L0_attn_hidden_states"].reshape(B * S, D)
    f["ident"] = np.eye(P, dtype=np.float32)
    j, i = np.arange(P)[:, None], np.arange(P)[None]
    f["masks"] = np.stack([((j >> (l + 1)) == (i >> (l + 1))) & ((j >> l) % 2 == 0) & ((i >> l) % 2 == 1)
                           for l in range(LV)], 1).astype(np.float32)
    a = lambda n: v["L0_attn_" + n]
    per_head = lambda w: w.reshape(H0, P, -1)
    cols = [transposed(a(n)).reshape(P, KD, H0, P).transpose(2, 0, 1, 3).reshape(H0, P, D) for n in ("Wq", "Wk", "Wv")]
    cols += [per_head(a(n)) for n in ("conv_q", "conv_k", "conv_v", "dt_bias")]
    cols += [np.broadcast_to(a("A_log")[:, None, None], (H0, P, 1)), per_head(a("bg2")), per_head(a("Wo").T),
             a("Wg2").reshape(H0, P, P).transpose(0, 2, 1)]
    f["headw"] = np.concatenate(cols, 2)
    f["wsvT"] = a("Wsv").T
    f["wg1T"] = transposed(a("Wg1"))
    f["norm_w"] = a("norm_w").reshape(P, 1)
    nets = np.stack([np.concatenate([a("Wb1")[:, e], a("Wa1")[:, e]]) for e in range(3)]
                    + [np.concatenate([a("bb1"), a("ba1")]), np.concatenate([a("Wb2")[0], a("Wa2")[0]])])
    f["mlp"] = np.broadcast_to(nets, (P, 5, 64))
    f["mb2"] = np.broadcast_to(np.concatenate([a("bb2"), a("ba2")]), (P, 2))
    l0, l1, l1f, l2, l2f, l3, l3f = [lambda n, pre=pre: v[pre + n] for pre in
                                     ("L0_ffn_", "L1_attn_", "L1_ffn_", "L2_attn_", "L2_ffn_", "L3_attn_", "L3_ffn_")]

    def up(parts, blocks):
        return np.stack([transposed(w).reshape(P, KD, blocks, -1).transpose(2, 0, 1, 3) for w in parts], 2).reshape(blocks, P, -1)

    def down(w, blocks):
        rows = w.T.reshape(blocks, -1, D)
        tiles = -(-rows.shape[1] // P)
        rows = np.concatenate([rows, np.zeros((blocks, tiles * P - rows.shape[1], D), w.dtype)], 1)
        return rows.reshape(blocks, tiles, P, D).transpose(0, 2, 1, 3).reshape(blocks, P, -1)

    on_all = lambda r: np.broadcast_to(r, (P,) + r.shape)
    f["w0all"] = np.stack([transposed(l0("w1")).reshape(P, -1), transposed(l0("w2")).reshape(P, -1), l0("w3").reshape(P, -1)], 1)
    f["f0w1"], f["f0w2"] = up([l0("w1"), l0("w2")], 2), down(l0("w3"), 2)
    heads = lambda w, n: transposed(w).reshape(P, KD, n, -1).transpose(2, 0, 1, 3)
    f["wq1"], f["wk1"], f["wv1"] = heads(l1("Wq"), H1), heads(l1("Wk"), KV1), heads(l1("Wv"), KV1)
    f["wo1"] = l1("Wo").T.reshape(H1, P, D)
    f["bo1"] = on_all(l1("bo"))
    f["causal"] = np.where(i <= j, 0.0, -1e30).astype(np.float32)
    gate_up = l1f("w_gate_up")
    f["f1w1"], f["f1w2"] = up([gate_up[:1024], gate_up[1024:]], 4), down(l1f("w_down"), 4)
    f["w2qkv"] = transposed(np.concatenate([l2("wq"), l2("wk"), l2("wv")], 1).T)
    f["b2qkv"] = on_all(np.concatenate([l2("bq"), l2("bk"), l2("bv")]))
    f["w2o"], f["b2o"] = transposed(l2("wo").T), on_all(l2("bo"))
    inv_freq = (1.0 / 1250 ** (np.arange(0, D2, 2, dtype=np.float32) / D2)).astype(np.float32)
    freqs = np.outer(np.arange(S, dtype=np.float32), inv_freq).astype(np.float32)
    by_tile = lambda t: t.astype(np.float32).reshape(QT, P, D2).transpose(1, 0, 2)
    f["cos"] = by_tile(np.concatenate([np.cos(freqs), np.cos(freqs)], 1))
    f["sin"] = by_tile(np.concatenate([-np.sin(freqs), np.sin(freqs)], 1))
    f["gate2"] = transposed(l2f("gate_weight"))
    f["q1"] = l2f("fc_up_qweights").reshape(E2, KD, P, P).transpose(0, 2, 1, 3).reshape(E2, P, -1)
    f["s1"] = np.repeat(l2f("fc_up_blocks_scale"), 16, 1).reshape(E2, KD, P, P).transpose(0, 2, 1, 3).reshape(E2, P, -1)
    f["q2"] = l2f("fc_down_qweights")
    f["s2"] = np.repeat(l2f("fc_down_blocks_scale"), 16, 1)
    f["gs"] = on_all(np.concatenate([l2f("fc_up_global_scale"), l2f("fc_down_global_scale")]))
    f["order"] = on_all(np.arange(16, 0, -1).astype(np.float32))
    qkv3 = l3("qkv_w").reshape(H3 // 2, 2, 3, D3, D)
    pair = lambda w: transposed(w.reshape(-1, D)).reshape(P, KD, H3 // 2, P).transpose(2, 0, 1, 3)
    q3, k3, v3, g3 = pair(qkv3[:, :, 0]), pair(qkv3[:, :, 1]), pair(qkv3[:, :, 2]), pair(l3("gate_w"))
    f["w3qk"] = np.stack([q3, k3, g3], 2).reshape(H3 // 2, P, -1)
    f["w3kv"] = np.concatenate([k3, v3], 3).reshape(H3 // 2, P, -1)
    f["w3o"] = l3("out_w").T.reshape(H3 // 2, P, D)
    f["w3nw"] = l3("norm_w").reshape(H3 // 2, P, 1)
    rate = (1.0 / 2.0 ** (8.0 / H3)) ** (np.arange(H3) + 1.0)
    slope = (rate * (1.0 + 1e-5)).reshape(H3 // 2, 1, 2, 1)
    gap = (i - j)[None, :, None, :]
    normal = lambda t: np.where(t < 1e-30, 0, t).astype(np.float32)
    f["w3dec"] = normal(np.where(gap >= 0, np.exp(-slope * np.maximum(gap, 0)), 0)).reshape(H3 // 2, P, -1)
    by_channel = np.repeat(slope.reshape(H3 // 2, 2), D3, 1)[:, :, None]
    f["w3qd"] = normal(np.exp(-by_channel * (np.arange(P) + 1)))
    f["w3kd"] = normal(np.exp(-by_channel.transpose(0, 2, 1) * (P - 1 - np.arange(P))[None, :, None]))
    f["w3cd"] = normal(np.exp(-by_channel * P))
    f["gate3"] = transposed(np.concatenate([l3f("router_w"), l3f("shared_gate_w")[None]]))
    f["fsw1"], f["fsw2"] = up([l3f("sw_gate").T, l3f("sw_up").T], 2), down(l3f("sw_down").T, 2)
    f["f3w1"] = np.stack([l3f(n).reshape(E3, KD, P, 176).transpose(0, 2, 1, 3) for n in ("w_gate", "w_up")], 2).reshape(E3, P, -1)
    f["f3w2"] = down(l3f("w_down").reshape(E3 * 176, D).T, E3)
    return {n: np.ascontiguousarray(x) for n, x in f.items()}


def kernel(**inputs):
    import concourse.bacc as bacc
    from concourse.bass_utils import run_bass_kernel_spmd

    nc = bacc.Bacc("TRN2", target_bir_lowering=False, num_devices=1)
    arrays = layout({n: np.asarray(x) for n, x in inputs.items()})
    ins = {n: nc.dram_tensor("in_" + n, x.shape, mybir.dt.from_np(x.dtype), kind="ExternalInput").ap()
           for n, x in arrays.items()}
    out = nc.dram_tensor("out", (B * S, D), F32, kind="ExternalOutput").ap()
    build_program(nc, ins, out, RUN)
    result = run_bass_kernel_spmd(nc, [{"in_" + n: x for n, x in arrays.items()}], core_ids=[0])
    return result.results[0]["out"].reshape(B, S, D)
```
